# Optimizing a Trainium2 kernel written in Bass

```python
import numpy as np
import jax
import jax.numpy as jnp

def _softmax(x, axis=-1):
    return jax.nn.softmax(x, axis=axis)

def _gelu(x):
    return jax.nn.gelu(x, approximate=True)

def _silu(x):
    return jax.nn.silu(x)

def _sigmoid(x):
    return jax.nn.sigmoid(x)

def _layernorm(x, axis=-1, eps=1e-05):
    m = jnp.mean(x, axis=axis, keepdims=True)
    v = jnp.var(x, axis=axis, keepdims=True)
    return (x - m) / jnp.sqrt(v + eps)

def _scatter_add(tgt, idx, src, axis=0):
    return tgt.at[idx].add(src)

def _segment_sum(src, seg, n):
    return jax.ops.segment_sum(src, seg, n)
kernel_name = 'mk_decoder_preln_d1_seqx_r8_d7a0a1'

def setup_inputs(seed: int=0):
    np.random.seed(seed)
    _w = jnp.asarray

    def _rec_inputs():
        import jax
        import jax.numpy as jnp
        _rk = jax.random.key(seed)
        x = 7.22e-05 + 1 * jax.random.normal(jax.random.fold_in(_rk, 1), (8, 128, 512), jnp.float32)
        _lenS = 128 - jax.random.randint(jax.random.fold_in(_rk, 7), (8,), 0, max(1, 128 // 4) + 1, jnp.int32)
        _lenS2 = 128 - jax.random.randint(jax.random.fold_in(_rk, 8), (8,), 0, max(1, 128 // 4) + 1, jnp.int32)
        _ctx_4096P = jax.random.normal(jax.random.fold_in(_rk, 11), (8, 16, 512), jnp.float32)
        _ctx_4096c = jax.random.dirichlet(jax.random.fold_in(_rk, 511), 0.3 * jnp.ones((16,), jnp.float32), (8, 128))
        _ctx_4096t = jnp.einsum('bsk,bkd->bsd', _ctx_4096c, _ctx_4096P)
        _ctx_4096t = _ctx_4096t * jax.lax.rsqrt(jnp.mean(jnp.square(_ctx_4096t)) + 1e-12) * 0.953939
        ctx_4096 = 4.13588e-05 + 0.999923 * (_ctx_4096t + 0.3 * jax.random.normal(jax.random.fold_in(_rk, 611), (8, 128, 512), jnp.float32))
        _validS = jnp.arange(128)[None, :] < _lenS[:, None]
        _validS2 = jnp.arange(128)[None, :] < _lenS2[:, None]
        _causal = jnp.tril(jnp.ones((128, 128), dtype=bool))
        mask_BxSxS2_bk0 = jnp.logical_not(jnp.broadcast_to(_validS2[:, None, :], (8, 128, 128)))
        return (x, ctx_4096, mask_BxSxS2_bk0)
    x, ctx_4096, mask_BxSxS2_bk0 = _rec_inputs()

    def _L0_attn_setup():
        import jax, jax.numpy as jnp
        import numpy as np
        import math
        D_MODEL = 256
        D_STATE = 16
        EXPAND = 2
        D_INNER = D_MODEL * EXPAND
        DT_RANK = math.ceil(D_MODEL / 16)
        BATCH, SEQ_LEN = (2, 64)
        key = jax.random.key(seed)
        ks = jax.random.split(key, 6)
        x = jax.random.normal(ks[0], (BATCH, SEQ_LEN, D_INNER), dtype=jnp.float32)
        A_log = jnp.log(jax.random.uniform(ks[1], (D_INNER, D_STATE), minval=0.5, maxval=16.0, dtype=jnp.float32))
        D = jnp.ones((D_INNER,), dtype=jnp.float32)
        x_proj_w = 0.02 * jax.random.normal(ks[2], (DT_RANK + 2 * D_STATE, D_INNER), dtype=jnp.float32)
        dt_init_std = DT_RANK ** (-0.5)
        dt_proj_w = jax.random.uniform(ks[3], (D_INNER, DT_RANK), minval=-dt_init_std, maxval=dt_init_std, dtype=jnp.float32)
        dt = jnp.exp(jax.random.uniform(ks[4], (D_INNER,), dtype=jnp.float32) * (math.log(0.1) - math.log(0.001)) + math.log(0.001))
        dt = jnp.clip(dt, 0.0001, None)
        dt_proj_b = dt + jnp.log(-jnp.expm1(-dt))
        return {'x': x, 'A_log': A_log, 'D': D, 'x_proj_w': x_proj_w, 'dt_proj_w': dt_proj_w, 'dt_proj_b': dt_proj_b}
    _L0_attn_all = _L0_attn_setup()
    _L0_attn_in = {k: v for k, v in _L0_attn_all.items() if k in ('A_log', 'D', 'x_proj_w', 'dt_proj_w', 'dt_proj_b')}
    del _L0_attn_all

    def _L0_xattn_setup():
        import jax, jax.numpy as jnp
        import numpy as np
        B, LQ, LK, D, H, DH = (2, 128, 128, 512, 32, 128)
        EPS = 1e-05

        def _rmsnorm(x, weight):
            var = jnp.mean(jnp.square(x), axis=-1, keepdims=True)
            return x * jax.lax.rsqrt(var + EPS) * weight
        key = jax.random.key(seed)
        ks = jax.random.split(key, 8)
        scale = 0.02
        return {'hidden_states': jax.random.normal(ks[0], (B, LQ, D), jnp.float32), 'key_value_states': jax.random.normal(ks[1], (B, LK, D), jnp.float32), 'attention_mask': jax.random.randint(ks[2], (B, LQ, LK), 0, 2) > 0, 'position_bias': jax.random.normal(ks[3], (H, LQ, LK), jnp.float32), 'ln_weight': jnp.ones((D,), jnp.float32), 'w_q': jax.random.normal(ks[4], (H * DH, D), jnp.float32) * scale, 'w_k': jax.random.normal(ks[5], (H * DH, D), jnp.float32) * scale, 'w_v': jax.random.normal(ks[6], (H * DH, D), jnp.float32) * scale, 'w_out': jax.random.normal(ks[7], (D, H * DH), jnp.float32) * scale}
    _L0_xattn_all = _L0_xattn_setup()
    _L0_xattn_in = {k: v for k, v in _L0_xattn_all.items() if k in ('position_bias', 'ln_weight', 'w_q', 'w_k', 'w_v', 'w_out')}
    del _L0_xattn_all

    def _L0_ffn_setup():
        import jax, jax.numpy as jnp
        import numpy as np
        B_SZ, S, D_IN, D_OUT = (4, 512, 512, 512)
        E, R = (16, 16)
        key = jax.random.key(seed)
        ks = jax.random.split(key, 6)
        x = jax.random.normal(ks[0], (B_SZ, S, D_IN), dtype=jnp.float32)
        W = jax.random.normal(ks[1], (D_OUT, D_IN), dtype=jnp.float32) * (1.0 / np.sqrt(D_IN))
        b = jax.random.normal(ks[2], (D_OUT,), dtype=jnp.float32) * 0.01
        A = jax.random.normal(ks[3], (E, R, D_IN), dtype=jnp.float32) * (1.0 / np.sqrt(D_IN))
        Bw = jax.random.normal(ks[4], (E, D_OUT, R), dtype=jnp.float32) * (1.0 / np.sqrt(R))
        probs = jax.random.uniform(ks[5], (E,), dtype=jnp.float32)
        probs = probs / jnp.sum(probs)
        return {'x': x, 'W': W, 'b': b, 'A': A, 'B': Bw, 'probs': probs}
    _L0_ffn_all = _L0_ffn_setup()
    _L0_ffn_in = {k: v for k, v in _L0_ffn_all.items() if k in ('W', 'b', 'A', 'B', 'probs')}
    del _L0_ffn_all
    return {'x': x, 'ctx_4096': ctx_4096, 'mask_BxSxS2_bk0': mask_BxSxS2_bk0, 'L0_attn_A_log': _L0_attn_in['A_log'], 'L0_attn_D': _L0_attn_in['D'], 'L0_attn_x_proj_w': _L0_attn_in['x_proj_w'], 'L0_attn_dt_proj_w': _L0_attn_in['dt_proj_w'], 'L0_attn_dt_proj_b': _L0_attn_in['dt_proj_b'], 'L0_xattn_position_bias': _L0_xattn_in['position_bias'], 'L0_xattn_ln_weight': _L0_xattn_in['ln_weight'], 'L0_xattn_w_q': _L0_xattn_in['w_q'], 'L0_xattn_w_k': _L0_xattn_in['w_k'], 'L0_xattn_w_v': _L0_xattn_in['w_v'], 'L0_xattn_w_out': _L0_xattn_in['w_out'], 'L0_ffn_W': _L0_ffn_in['W'], 'L0_ffn_b': _L0_ffn_in['b'], 'L0_ffn_A': _L0_ffn_in['A'], 'L0_ffn_B': _L0_ffn_in['B'], 'L0_ffn_probs': _L0_ffn_in['probs']}

def reference(x, ctx_4096, mask_BxSxS2_bk0, L0_attn_A_log, L0_attn_D, L0_attn_x_proj_w, L0_attn_dt_proj_w, L0_attn_dt_proj_b, L0_xattn_position_bias, L0_xattn_ln_weight, L0_xattn_w_q, L0_xattn_w_k, L0_xattn_w_v, L0_xattn_w_out, L0_ffn_W, L0_ffn_b, L0_ffn_A, L0_ffn_B, L0_ffn_probs):
    import jax
    import jax.numpy as jnp

    def _L0_attn_ref(x, A_log, D, x_proj_w, dt_proj_w, dt_proj_b):
        import jax, jax.numpy as jnp
        import numpy as np
        import math
        D_MODEL = 256
        D_STATE = 16
        EXPAND = 2
        D_INNER = D_MODEL * EXPAND
        DT_RANK = math.ceil(D_MODEL / 16)
        BATCH, SEQ_LEN = (2, 64)
        A = -jnp.exp(A_log)
        xp = jnp.einsum('bld,rd->blr', x, x_proj_w)
        dt_in = xp[..., :DT_RANK]
        B = xp[..., DT_RANK:DT_RANK + D_STATE]
        C = xp[..., DT_RANK + D_STATE:]
        dt = jax.nn.softplus(jnp.einsum('blr,dr->bld', dt_in, dt_proj_w) + dt_proj_b)
        dA = jnp.exp(dt[..., None] * A)
        dBx = dt[..., None] * B[:, :, None, :] * x[..., None]

        def step(h, inp):
            dA_t, dBx_t, C_t = inp
            h = dA_t * h + dBx_t
            y = jnp.einsum('bdn,bn->bd', h, C_t)
            return (h, y)
        h0 = jnp.zeros((x.shape[0], D_INNER, D_STATE), dtype=x.dtype)
        _, ys = jax.lax.scan(step, h0, (jnp.moveaxis(dA, 1, 0), jnp.moveaxis(dBx, 1, 0), jnp.moveaxis(C, 1, 0)))
        y = jnp.moveaxis(ys, 0, 1) + D * x
        return y

    def _L0_xattn_ref(hidden_states, key_value_states, attention_mask, position_bias, ln_weight, w_q, w_k, w_v, w_out):
        import jax, jax.numpy as jnp
        import numpy as np
        B, LQ, LK, D, H, DH = (2, 128, 128, 512, 32, 128)
        EPS = 1e-05

        def _rmsnorm(x, weight):
            var = jnp.mean(jnp.square(x), axis=-1, keepdims=True)
            return x * jax.lax.rsqrt(var + EPS) * weight
        x = _rmsnorm(hidden_states, ln_weight)
        b, lq, _ = x.shape
        lk = key_value_states.shape[1]
        h_q = (x @ w_q.T).reshape(b, lq, H, DH)
        h_k = (key_value_states @ w_k.T).reshape(b, lk, H, DH)
        h_v = (key_value_states @ w_v.T).reshape(b, lk, H, DH)
        score = jnp.einsum('bqhd,bkhd->bhqk', h_q, h_k)
        score = score + position_bias[None]
        m = attention_mask[:, None]
        score = jnp.where(m, score, -jnp.inf)
        score = jax.nn.softmax(score, axis=-1)
        score = jnp.where(m, score, 0.0)
        attn = jnp.einsum('bhqk,bkhd->bqhd', score, h_v).reshape(b, lq, H * DH)
        out = attn @ w_out.T
        return hidden_states + out

    def _L0_ffn_ref(x, W, b, A, B, probs):
        import jax, jax.numpy as jnp
        import numpy as np
        B_SZ, S, D_IN, D_OUT = (4, 512, 512, 512)
        E, R = (16, 16)
        out = jnp.einsum('bsd,od->bso', x, W) + b
        h = jnp.einsum('bsd,erd->bser', x, A)
        contrib = jnp.einsum('bser,e,eor->bso', h, probs, B)
        return out + contrib
    x = x + _L0_attn_ref(_layernorm(x, axis=-1), L0_attn_A_log, L0_attn_D, L0_attn_x_proj_w, L0_attn_dt_proj_w, L0_attn_dt_proj_b)
    x = x + _L0_xattn_ref(_layernorm(x, axis=-1), ctx_4096, mask_BxSxS2_bk0, L0_xattn_position_bias, L0_xattn_ln_weight, L0_xattn_w_q, L0_xattn_w_k, L0_xattn_w_v, L0_xattn_w_out)
    x = x + _L0_ffn_ref(_layernorm(x, axis=-1), L0_ffn_W, L0_ffn_b, L0_ffn_A, L0_ffn_B, L0_ffn_probs)
    return x

_drawn_inputs = setup_inputs


def setup_inputs(seed=0):
    import zlib

    import numpy as np

    out = dict(_drawn_inputs(seed))
    spreads = {'L0_attn_D': (1.0, 0.2), 'L0_xattn_ln_weight': (1.0, 0.6)}
    factors = {'L0_attn_A_log': 5.424,
     'L0_attn_x_proj_w': 2.738,
     'L0_attn_dt_proj_w': 8.0,
     'L0_attn_dt_proj_b': 3.828,
     'L0_ffn_b': 29.916,
     'L0_ffn_probs': 3.138}
    for name, (base, spread) in spreads.items():
        noise = np.random.default_rng([zlib.crc32(name.encode()), seed]).standard_normal(out[name].shape)
        drawn = base * np.exp(spread * noise) if base else spread * noise
        out[name] = jnp.asarray(drawn.astype(out[name].dtype))
    for name, factor in factors.items():
        out[name] = (out[name] * factor).astype(out[name].dtype)
    return out
```

```python
from contextlib import ExitStack

import concourse.bass as bass
from concourse import mybir

F32 = mybir.dt.float32
F32R = mybir.dt.float32r
BF16 = mybir.dt.bfloat16
U8 = mybir.dt.uint8
ALU = mybir.AluOpType
ACT = mybir.ActivationFunctionType
AX_X = mybir.AxisListType.X

P = 128
B = 8
S = 128
D = 512
C = D // P
T = B * S
H = 32
N = 16
R = 16
RX = R + 2 * N
G = 4
NG = H // G
HB = B // 2
HT = HB * S
KP = 2 * G
STEPS = 2 * H
TRI = 3
LAST_TRI = N // TRI
J = TRI * C
E = 16
ER = E * 16 // P
EPS = 1e-5
MASKED = -1e30


def decoder_layer(nc, a):
    k_dram = nc.dram_tensor("k_scratch", (STEPS, P, HT), F32, kind="Internal").ap()
    v_dram = nc.dram_tensor("v_scratch", (STEPS, P, HT), F32, kind="Internal").ap()
    xp_dram = nc.dram_tensor("xp_scratch", (2, N, T), F32, kind="Internal").ap()
    v_dram_g = v_dram.rearrange("(q h) p x -> q p h x", h=G)

    with ExitStack() as whole:
        def sb(stack, name, shape, dt=F32, side="left"):
            return stack.enter_context(nc.sbuf_tensor(name, shape, dt, side=side))

        acc = whole.enter_context(nc.psum_tensor("acc", [P, 4, 512], F32))
        misc = whole.enter_context(nc.psum_tensor("misc", [P, 4, 512], F32))
        psQ, psS, psT, psO = (misc[:, i, :] for i in range(4))

        base = sb(whole, "base", [P, B, D])
        ident = sb(whole, "ident", [P, P])
        identb = sb(whole, "identb", [P, P], BF16)
        maskadd = sb(whole, "maskadd", [P, B, S], BF16)
        anykey = sb(whole, "anykey", [P, B])
        lnw = sb(whole, "lnw", [P, C])
        stats = sb(whole, "stats", [P, B, 6])
        mv = sb(whole, "mv", [P, B, 2])
        var = sb(whole, "var", [P, B])
        rstd = sb(whole, "rstd", [P, B])
        tmp8 = sb(whole, "tmp8", [P, B])

        with ExitStack() as low:
            ctx_hi = sb(low, "ctx_hi", [P, C, T], F32R, "right")
            ctx_lo = sb(low, "ctx_lo", [P, C, T], F32R, "right")
            wraw = sb(low, "wraw", [P, C, G * P], F32, "right")
            wk_hi = sb(low, "wk_hi", [P, C, G * P], F32R, "right")
            wk_lo = sb(low, "wk_lo", [P, C, G * P], F32R, "right")
            wv_hi = sb(low, "wv_hi", [P, C, G * P], F32R, "right")
            wv_lo = sb(low, "wv_lo", [P, C, G * P], F32R, "right")
            kst = [sb(low, f"kst{i}", [P, HT], F32, "right") for i in range(2)]
            vst = [sb(low, f"vst{i}", [P, G, 2, P], F32, "right") for i in range(2)]

        with ExitStack() as tail:
            zf_hi = sb(tail, "zf_hi", [P, C, T], F32R, "right")
            zf_lo = sb(tail, "zf_lo", [P, C, T], F32R, "right")
            ffn_w = sb(tail, "ffn_w", [P, C, D], F32, "right")
            weff_hi = sb(tail, "weff_hi", [P, C, D], F32R, "right")
            weff_lo = sb(tail, "weff_lo", [P, C, D], F32R, "right")
            ea_sb = sb(tail, "ea_sb", [P, ER, D], F32, "right")
            eb_sb = sb(tail, "eb_sb", [P, ER, D], F32, "right")
            eprob = sb(tail, "eprob", [P, ER], F32, "right")
            ffn_b = sb(tail, "ffn_b", [P, D], F32, "right")
            xn = sb(tail, "xn", [P, B, D], F32, "right")

        with ExitStack() as scan:
            dt_ = sb(scan, "dt_", [P, C, T])
            u = sb(scan, "u", [P, C, T])
            bc = [sb(scan, f"bc{i}", [P, 2, T]) for i in range(TRI)]
            dA = [sb(scan, f"dA{i}", [P, B, S]) for i in range(2)]
            y = sb(scan, "y", [P, C, T])
            w = sb(scan, "w", [P, C, T])
            negA = sb(scan, "negA", [P, C, N])
            dskip = sb(scan, "dskip", [P, C])
            dtb = sb(scan, "dtb", [P, C])
            xpw = sb(scan, "xpw", [P, C, RX])
            dtw = sb(scan, "dtw", [R, D])
            maskraw = sb(scan, "maskraw", [P, B, S], U8)

        pair = range(2)
        z_hi = sb(whole, "z_hi", [P, C, T], F32R)
        z_lo = sb(whole, "z_lo", [P, C, T], F32R)
        wq_raw = [sb(whole, f"wq_raw{i}", [P, C, P]) for i in pair]
        wq_hi = [sb(whole, f"wq_hi{i}", [P, C, P], F32R) for i in pair]
        wq_lo = [sb(whole, f"wq_lo{i}", [P, C, P], F32R) for i in pair]
        wo_raw = [sb(whole, f"wo_raw{i}", [P, D]) for i in pair]
        wo_hi = [sb(whole, f"wo_hi{i}", [P, D], F32R) for i in pair]
        wo_lo = [sb(whole, f"wo_lo{i}", [P, D], F32R) for i in pair]
        k_sb = [sb(whole, f"k_sb{i}", [P, HT]) for i in pair]
        v_sb = [sb(whole, f"v_sb{i}", [P, HB, P]) for i in pair]
        q_sb = [sb(whole, f"q_sb{i}", [P, HT]) for i in pair]
        prob = [sb(whole, f"prob{i}", [P, HB, S]) for i in pair]
        pt_sb = [sb(whole, f"pt_sb{i}", [P, HB, S]) for i in pair]
        bias = [sb(whole, f"bias{i}", [P, S]) for i in pair]
        negm = [sb(whole, f"negm{i}", [P, HB]) for i in pair]
        psum = [sb(whole, f"psum{i}", [P, HB]) for i in pair]
        rec = [sb(whole, f"rec{i}", [P, HB]) for i in pair]
        ot_hi = [sb(whole, f"ot_hi{i}", [P, HT], F32R) for i in pair]
        ot_lo = [sb(whole, f"ot_lo{i}", [P, HT], F32R) for i in pair]

        w_tok = w[:, :, :].rearrange("p c (h d) -> p (c h) d", d=D)
        xp_sb = base[:, 0:2, :].rearrange("p h t -> p (h t)")
        ctx_raw = base[:, :, :].rearrange("p (c h) t -> p c (h t)", c=C)

        def sem(name):
            return whole.enter_context(nc.semaphore(name))

        x_in = [sem(f"x_in{i}") for i in range(2)]
        ctx_in = [sem(f"ctx_in{i}") for i in range(C)]
        params_in, x_again, wraw_in = sem("params_in"), sem("x_again"), sem("wraw_in")
        k_stored = [sem(f"k_stored{i}") for i in range(2)]
        v_stored = [sem(f"v_stored{i}") for i in range(2)]
        xp_stored = sem("xp_stored")
        bc_in = [sem(f"bc_in{i}") for i in range(TRI)]
        wq_in = [sem(f"wq_in{i}") for i in pair]
        wo_in = [sem(f"wo_in{i}") for i in pair]
        kb_in = [sem(f"kb_in{i}") for i in pair]
        v_in = [sem(f"v_in{i}") for i in pair]
        ffn_in, out_stored = sem("ffn_in"), sem("out_stored")
        ident_set, ident_done, mask_done = sem("ident_set"), sem("ident_done"), sem("mask_done")
        ctx_hi_done, ctx_lo_done = sem("ctx_hi_done"), sem("ctx_lo_done")
        w_hi_done, w_lo_done = sem("w_hi_done"), sem("w_lo_done")
        k_done, k_evac, v_done, v_evac = sem("k_done"), sem("k_evac"), sem("v_done"), sem("v_evac")
        ln_var, ln_log, ln_exp = sem("ln_var"), sem("ln_log"), sem("ln_exp")
        ln1_done = sem("ln1_done")
        xt_ps, xt_evac, xp_ps, xp_evac, dt_ps = sem("xt_ps"), sem("xt_evac"), sem("xp_ps"), sem("xp_evac"), sem("dt_ps")
        sp_abs, sp_exp, sp_log, sp_done = sem("sp_abs"), sem("sp_exp"), sem("sp_log"), sem("sp_done")
        a_exp, a_neg = sem("a_exp"), sem("a_neg")
        y_ready, da_free, da_ready = sem("y_ready"), sem("da_free"), sem("da_ready")
        dbx_done, prod_done = sem("dbx_done"), sem("prod_done")
        yt_ps, x1_done, zn_done, zt_ps = sem("yt_ps"), sem("x1_done"), sem("zn_done"), sem("zt_ps")
        z_hi_done, z_lo_done = sem("z_hi_done"), sem("z_lo_done")
        wq_hi_done, wq_lo_done = sem("wq_hi_done"), sem("wq_lo_done")
        wo_hi_done, wo_lo_done = sem("wo_hi_done"), sem("wo_lo_done")
        q_done, q_evac, s_done, sb_done = sem("q_done"), sem("q_evac"), sem("s_done"), sem("sb_done")
        mx_done, exp_done, rec_done, recv_done = sem("mx_done"), sem("exp_done"), sem("rec_done"), sem("recv_done")
        p_ready, t_done, pt_evac, pv_done = sem("p_ready"), sem("t_done"), sem("pt_evac"), sem("pv_done")
        ot_hi_done, ot_lo_done, o_done, x2_done = sem("ot_hi_done"), sem("ot_lo_done"), sem("o_done"), sem("x2_done")
        eb_done, weff_ps, weff_sum = sem("eb_done"), sem("weff_ps"), sem("weff_sum")
        weff_hi_done, weff_lo_done = sem("weff_hi_done"), sem("weff_lo_done")
        ln3_done, zf_ps = sem("ln3_done"), sem("zf_ps")
        zf_hi_done, zf_lo_done, f_done, out_ready = sem("zf_hi_done"), sem("zf_lo_done"), sem("f_done"), sem("out_ready")
        dve_chain = sem("dve_chain")

        block = whole.enter_context(nc.Block())

        def pipeline(eng, step):
            for g in range(4):
                step(g, g, 0)
            with eng.Fori(2, H // 2 - 1) as i:
                for p in pair:
                    step(2 * i + p, p, 0)
            for g in range(H - 2, H + 4):
                step(g, g, g // H)
            with eng.Fori(H // 2 + 2, H - 1) as i:
                for p in pair:
                    step(2 * i + p, p, 1)
            for g in range(STEPS - 2, STEPS + 3):
                step(g, g, 1)

        def known(g):
            return isinstance(g, int)

        def runs(g):
            return not known(g) or 0 <= g < STEPS

        def in_count(g, p, n):
            return n * (g // 2 + 1) if known(g) else n // 2 * (g - p) + n

        @block.sync
        def _(sp):
            sp.dma_start(wraw[:], a["wk"][0]).then_inc(wraw_in, 16)
            for c in range(C):
                sp.dma_start(ctx_raw[:, c], a["ctxT"][:, c]).then_inc(ctx_in[c], 16)
            for i in range(2):
                sp.dma_start(w_tok[:, HB * i:HB * (i + 1)],
                             a["x"][HB * i:HB * (i + 1)].rearrange("b t d -> t b d")).then_inc(x_in[i], 16)
            for dst, src in ((negA, "A_log"), (dskip, "D"), (dtb, "dt_b"), (xpw, "xp_w"), (dtw, "dt_w"), (lnw, "ln_w")):
                sp.dma_start(dst[:], a[src]).then_inc(params_in, 16)
            sp.dma_start(maskraw[:], a["mask"].rearrange("b q k -> q b k")).then_inc(params_in, 16)

            def k_store(g, j):
                sp.wait_ge(k_evac, KP * g + j + 1)
                sp.dma_start(k_dram[H * (j % 2) + G * g + j // 2], kst[j % 2][:]).then_inc(k_stored[j % 2], 16)

            def v_store(g, q):
                sp.wait_ge(v_evac, B * g + 2 * q + 2)
                sp.dma_start(v_dram_g[NG * (q // 2) + g, :, :, 2 * P * (q % 2):2 * P * (q % 2 + 1)],
                             vst[q % 2][:, :, :, :].rearrange("p h b d -> p h (b d)")).then_inc(v_stored[q % 2], 16)

            def group(g, more):
                for j in range(KP):
                    k_store(g, j)
                    if more and j == 2:
                        sp.wait_ge(w_lo_done, 2 * g + 2)
                        sp.dma_start(wraw[:], a["wk"][g + 1]).then_inc(wraw_in, 16)
                for q in range(4):
                    v_store(g, q)
                    if more and q == 1:
                        sp.wait_ge(w_lo_done, 2 * g + 3)
                        sp.dma_start(wraw[:], a["wv"][g + 1]).then_inc(wraw_in, 16)

            sp.wait_ge(w_lo_done, 1)
            sp.dma_start(wraw[:], a["wv"][0]).then_inc(wraw_in, 16)
            group(0, True)
            sp.wait_ge(dt_ps, C)
            sp.wait_ge(xp_stored, 16)
            sp.dma_start(base[:], a["x"].rearrange("b t d -> t b d")).then_inc(x_again, 16)
            with sp.Fori(1, NG - 1) as g:
                group(g, True)

            def load_wq(h, p):
                sp.dma_start(wq_raw[p][:], a["wq"][h]).then_inc(wq_in[p], 16)

            def load_kb(g, h, p):
                sp.dma_start(k_sb[p][:], k_dram[g]).then_inc(kb_in[p], 16)
                sp.dma_start(bias[p][:], a["pbias"][h]).then_inc(kb_in[p], 16)

            sp.wait_ge(prod_done, C * N)
            for g in range(2):
                load_wq(g, g)
            group(NG - 1, False)
            for i in range(2):
                sp.wait_ge(k_stored[i], 16 * KP // 2 * NG)
                sp.wait_ge(v_stored[i], 16 * 2 * NG)
            sp.wait_ge(yt_ps, B)
            load_kb(0, 0, 0)
            sp.wait_ge(v_done, B * NG)
            sp.dma_start(ffn_w[:], a["ffn_w"]).then_inc(ffn_in, 16)
            sp.dma_start(ea_sb[:], a["ffn_a"]).then_inc(ffn_in, 16)
            sp.dma_start(eb_sb[:], a["ffn_bw"]).then_inc(ffn_in, 16)
            sp.dma_start(ffn_b[:], a["ffn_b"].partition_broadcast(P)).then_inc(ffn_in, 16)
            for e in range(ER):
                sp.dma_start(eprob[:, e:e + 1], a["probs"][P * e:P * (e + 1), :]).then_inc(ffn_in, 16)

            def head(g, half):
                return g % H if known(g) else g - H * half

            def step(g, par, half):
                p = par % 2
                if runs(g) and runs(g + 2):
                    if not known(g) or g >= 0:
                        sp.wait_ge(wq_lo_done, g + 1)
                    load_wq(head(g + 2, half), p)
                if runs(g) and runs(g + 1):
                    if not known(g) or g >= 1:
                        sp.wait_ge(sb_done, g)
                    load_kb(g + 1, head(g + 1, half), 1 - p)
                if runs(g):
                    if not known(g) or g >= 2:
                        sp.wait_ge(pv_done, g - 1)
                    sp.dma_start(v_sb[p][:, :, :].rearrange("p b d -> p (b d)"), v_dram[g]).then_inc(v_in[p], 16)
                    if not known(g) or g >= 2:
                        sp.wait_ge(wo_lo_done, g - 1)
                    sp.dma_start(wo_raw[p][:], a["wo"][head(g, half)]).then_inc(wo_in[p], 16)

            pipeline(sp, step)
            for b in range(B):
                sp.wait_ge(out_ready, b + 1)
                sp.dma_start(a["out"][b], base[:, b]).then_inc(out_stored, 16)
            sp.wait_ge(out_stored, 16 * B)

        @block.tensor
        def _(pe):
            def three(out, w_hi, w_lo, m_hi, m_lo, first, last):
                pe.matmul(out, w_hi, m_hi, start=first, stop=False)
                pe.matmul(out, w_hi, m_lo, start=False, stop=False)
                return pe.matmul(out, w_lo, m_hi, start=False, stop=last)

            def k_sum(g, j, first=False):
                if not first or j >= 2:
                    pe.wait_ge(k_evac, KP * g + j - 1)
                hd, half = slice(j // 2 * P, (j // 2 + 1) * P), slice(j % 2 * HT, (j % 2 + 1) * HT)
                for c in range(C):
                    if first and j == 0:
                        pe.wait_ge(ctx_lo_done, c + 1)
                    mm = three(acc[:, j % 2], wk_hi[:, c, hd], wk_lo[:, c, hd], ctx_hi[:, c, half], ctx_lo[:, c, half],
                               c == 0, c == C - 1)
                mm.then_inc(k_done, 1)

            def v_sum(g, b, first=False):
                if not first or b >= 2:
                    pe.wait_ge(v_evac, B * g + b - 1)
                tok = slice(b * S, (b + 1) * S)
                for c in range(C):
                    mm = three(acc[:, 2 + b % 2], ctx_hi[:, c, tok], ctx_lo[:, c, tok], wv_hi[:, c], wv_lo[:, c],
                               c == 0, c == C - 1)
                mm.then_inc(v_done, 1)

            pe.wait_ge(w_lo_done, 1)
            for j in range(2):
                k_sum(0, j, True)
            pe.wait_ge(ident_done, 2)
            for c in range(C):
                if c >= 2:
                    pe.wait_ge(xt_evac, c - 1)
                for b in range(B):
                    if c == 0:
                        pe.wait_ge(ln1_done, b + 1)
                    mm = pe.transpose(misc[:, 2 * (c % 2) + b // HB, b % HB * S:(b % HB + 1) * S],
                                      w_tok[:, b, c * P:(c + 1) * P], ident[:])
                mm.then_inc(xt_ps, 1)
            for j in range(2, 4):
                k_sum(0, j, True)
            pe.wait_ge(params_in, 16 * 7)
            pe.wait_ge(xt_evac, C)
            for half in range(2):
                for c in range(C):
                    mm = pe.matmul(misc[0:RX, half], xpw[:, c], y[:, c, half * HT:(half + 1) * HT],
                                   start=(c == 0), stop=(c == C - 1))
            mm.then_inc(xp_ps, 1)
            for j in range(4, 6):
                k_sum(0, j, True)
            pe.wait_ge(xp_evac, 1)
            for c in range(C):
                if c >= 2:
                    pe.wait_ge(sp_abs, c - 1)
                    pe.wait_ge(sp_done, 2 * c - 3)
                for half in range(2):
                    mm = pe.matmul(misc[:, 2 * (c % 2) + half], dtw[:, c * P:(c + 1) * P],
                                   xp_sb[0:R, half * HT:(half + 1) * HT], start=True, stop=True)
                mm.then_inc(dt_ps, 1)
                if c == 1:
                    for j in range(6, KP):
                        k_sum(0, j, True)
            pe.wait_ge(w_lo_done, 2)
            for b in range(B):
                v_sum(0, b, True)

            def group(g):
                pe.wait_ge(w_lo_done, 2 * g + 1)
                for j in range(KP):
                    k_sum(g, j)
                pe.wait_ge(w_lo_done, 2 * g + 2)
                for b in range(B):
                    v_sum(g, b)

            with pe.Fori(1, NG - 1) as g:
                group(g)

            pe.wait_ge(y_ready, C * N + C)
            for b in range(B):
                if b >= 4:
                    pe.wait_ge(x1_done, b - 3)
                for c in range(C):
                    mm = pe.transpose(misc[:, b % 4, c * P:(c + 1) * P], y[:, c, b * S:(b + 1) * S], ident[:])
                mm.then_inc(yt_ps, 1)
            g = NG - 1
            pe.wait_ge(w_lo_done, 2 * g + 1)
            for j in range(KP):
                k_sum(g, j)
            pe.wait_ge(w_lo_done, 2 * g + 2)
            for b in range(3):
                v_sum(g, b)
            for c in range(C):
                if c >= 2:
                    pe.wait_ge(z_lo_done, c - 1)
                for b in range(B):
                    if c == 0:
                        pe.wait_ge(zn_done, b + 1)
                    mm = pe.transpose(misc[:, 2 * (c % 2) + b // HB, b % HB * S:(b % HB + 1) * S],
                                      w_tok[:, b, c * P:(c + 1) * P], ident[:])
                mm.then_inc(zt_ps, 1)
                v_sum(g, 3 + c)
            v_sum(g, 3 + C)
            pe.wait_ge(z_lo_done, C)
            pe.wait_ge(mask_done, 1)

            def step(g, par, half):
                p = par % 2
                if runs(g):
                    tok = slice(half * HT, (half + 1) * HT)
                    pe.wait_ge(wq_lo_done, g + 1)
                    if not known(g) or g:
                        pe.wait_ge(q_evac, g)
                    for c in range(C):
                        mm = three(psQ, wq_hi[p][:, c], wq_lo[p][:, c], z_hi[:, c, tok], z_lo[:, c, tok],
                                   c == 0, c == C - 1)
                    mm.then_inc(q_done, 1)
                if runs(g - 2):
                    pe.wait_ge(p_ready, g - 1)
                    if not known(g) or g > 2:
                        pe.wait_ge(pt_evac, g - 2)
                    for b in range(HB):
                        mm = pe.transpose(psT[:, b * S:(b + 1) * S], prob[p][:, b], ident[:])
                    mm.then_inc(t_done, 1)
                if runs(g - 1):
                    sh = (g - 1) // H if known(g) else half
                    pe.wait_ge(q_evac, g)
                    pe.wait_ge(kb_in[1 - p], in_count(g - 1, 1 - p, 32))
                    if not known(g) or g > 1:
                        pe.wait_ge(sb_done, g - 1)
                    pe.matmul(psS, identb[:], maskadd[:, sh * HB:(sh + 1) * HB, :].rearrange("p b k -> p (b k)"),
                              start=True, stop=False, skip_group_check=True)
                    for b in range(HB):
                        mm = pe.matmul(psS[:, b * S:(b + 1) * S], q_sb[1 - p][:, b * S:(b + 1) * S],
                                       k_sb[1 - p][:, b * S:(b + 1) * S], start=False, stop=(b == HB - 1),
                                       skip_group_check=True)
                    mm.then_inc(s_done, 1)
                if runs(g - 2):
                    pe.wait_ge(pt_evac, g - 1)
                    pe.wait_ge(v_in[p], in_count(g - 2, p, 16))
                    if not known(g) or g > 2:
                        pe.wait_ge(ot_lo_done, g - 2)
                    for b in range(HB):
                        mm = pe.matmul(psO[:, b * S:(b + 1) * S], v_sb[p][:, b], pt_sb[p][:, b], start=True, stop=True)
                    mm.then_inc(pv_done, 1)
                if runs(g - 3):
                    h = (g - 3) % H if known(g) else 1
                    q = 1 - p
                    if known(g) and g == 3:
                        pe.wait_ge(k_evac, KP * NG)
                        pe.wait_ge(v_evac, B * NG)
                    pe.wait_ge(ot_lo_done, g - 2)
                    pe.wait_ge(wo_lo_done, g - 2)
                    for b in range(HB):
                        tok = slice(b * S, (b + 1) * S)
                        if known(g) and g - 3 == H:
                            pe.wait_ge(x2_done, b + 1)
                        mm = three(acc[:, b], ot_hi[q][:, tok], ot_lo[q][:, tok], wo_hi[q][:], wo_lo[q][:],
                                   h == 0, h == H - 1)
                    mm.then_inc(o_done, 1)

            pipeline(pe, step)

            pe.wait_ge(eb_done, ER)
            pe.wait_ge(ot_lo_done, STEPS)
            for c in range(C):
                for e in range(ER):
                    mm = pe.matmul(misc[:, c], ea_sb[:, e, c * P:(c + 1) * P], eb_sb[:, e], start=(e == 0), stop=(e == ER - 1))
                mm.then_inc(weff_ps, 1)
            for half in range(2):
                for c in range(C):
                    if half == 0:
                        pe.wait_ge(weff_sum, c + 1)
                    else:
                        pe.wait_ge(zf_lo_done, c + 1)
                    for b in range(HB):
                        if c == 0:
                            pe.wait_ge(ln3_done, half * HB + b + 1)
                        mm = pe.transpose(misc[:, c, b * S:(b + 1) * S], xn[:, half * HB + b, c * P:(c + 1) * P], ident[:])
                    mm.then_inc(zf_ps, 1)
                if half == 0:
                    pe.wait_ge(weff_lo_done, C)
                for b in range(half * HB, (half + 1) * HB):
                    if half == 0:
                        pe.wait_ge(x2_done, HB + b + 1)
                    else:
                        pe.wait_ge(out_ready, b - HB + 1)
                    tok = slice(b * S, (b + 1) * S)
                    for c in range(C):
                        if b == half * HB:
                            pe.wait_ge(zf_lo_done, C * half + c + 1)
                        mm = three(acc[:, b % HB], zf_hi[:, c, tok], zf_lo[:, c, tok], weff_hi[:, c], weff_lo[:, c],
                                   c == 0, c == C - 1)
                    mm.then_inc(f_done, 1)

        @block.scalar
        def _(act):
            def inverse_root(n, part):
                act.wait_ge(ln_var, n)
                act.activation(tmp8[:, part], var[:, part], ACT.Ln).then_inc(ln_log, 1)
                act.wait_ge(ln_log, n)
                act.activation(rstd[:, part], tmp8[:, part], ACT.Exp, scale=-0.5).then_inc(ln_exp, 1)

            def split_w(m, hi):
                act.wait_ge(wraw_in, 16 * (m + 1))
                act.activation(hi[:], wraw[:], ACT.Copy).then_inc(w_hi_done, 1)

            def k_copy(g, j, first=False):
                act.wait_ge(k_done, KP * g + j + 1)
                if not first or j >= 2:
                    act.wait_ge(k_stored[j % 2], 16 * (KP // 2 * g + j // 2))
                act.activation(kst[j % 2][:], acc[:, j % 2], ACT.Copy).then_inc(k_evac, 1)

            def v_copy(g, b, first=False):
                act.wait_ge(v_done, B * g + b + 1)
                q = b // 2
                if not first or q >= 2:
                    act.wait_ge(v_stored[q % 2], 16 * (2 * g + q // 2))
                act.activation(vst[q % 2][:, :, b % 2], acc[:, 2 + b % 2].rearrange("p (h d) -> p h d", d=P),
                               ACT.Copy).then_inc(v_evac, 1)

            def dA_exp(g, t, c):
                j = J * (g - 1) + C * t + c
                act.wait_ge(da_free, j + 1)
                n = TRI * (g - 1) + t
                act.activation(dA[c % 2][:, :, 1:S], dt_[:, c].rearrange("p (b s) -> p b s", s=S)[:, :, 1:S],
                               ACT.Exp, scale=negA[:, c, bass.ds(n, 1)] if not known(n) else negA[:, c, n:n + 1]
                               ).then_inc(da_ready, 1)

            def load_bc(n, i):
                act.dma_start(bc[i][:], xp_dram[:, n].partition_broadcast(P)).then_inc(bc_in[i], 16)

            def group(g, steps, bc_loads):
                act.wait_ge(v_done, B * g)
                split_w(2 * g + 1, wv_hi)
                copies = [(k_copy, j) for j in range(KP)] + [(v_copy, b) for b in range(B)]
                for i, (copy, j) in enumerate(copies):
                    if i == KP:
                        act.wait_ge(k_done, KP * g + KP)
                        split_w(2 * g + 2, wk_hi)
                    if i % 4 != 3 and steps:
                        t, c = steps.pop(0)
                        dA_exp(g, t, c)
                        if c == C - 1 and t < bc_loads:
                            load_bc(TRI * (g - 1) + t + 2, (t + 2) % TRI)
                    copy(g, j)

            def all_steps(states):
                return [(t, c) for t in range(states) for c in range(C)]

            act.wait_ge(wraw_in, 16)
            act.activation(wk_hi[:], wraw[:], ACT.Copy).then_inc(w_hi_done, 1)
            for c in range(C):
                act.wait_ge(ctx_in[c], 16)
                act.activation(ctx_hi[:, c], ctx_raw[:, c], ACT.Copy).then_inc(ctx_hi_done, 1)
            act.wait_ge(params_in, 16 * 7)
            act.activation(negA[:], negA[:], ACT.Exp).then_inc(a_exp, 1)
            act.wait_ge(a_exp, 1)
            act.activation(negA[:], negA[:], ACT.Copy, scale=-1.0).then_inc(a_neg, 1)
            split_w(1, wv_hi)
            inverse_root(1, slice(0, B))
            for j in range(2):
                k_copy(0, j, True)
            for c in range(C):
                act.wait_ge(xt_ps, c + 1)
                act.activation(y[:, c].rearrange("p (h t) -> p h t", t=HT), misc[:, 2 * (c % 2):2 * (c % 2) + 2],
                               ACT.Copy).then_inc(xt_evac, 1)
            for j in range(2, 4):
                k_copy(0, j, True)
            act.wait_ge(xp_ps, 1)
            act.activation(xp_sb[0:RX, :].rearrange("p (h t) -> p h t", t=HT), misc[0:RX, 0:2], ACT.Copy).then_inc(xp_evac, 1)
            act.wait_ge(xp_evac, 1)
            act.dma_start(xp_dram.rearrange("a n t -> (a n) t"), xp_sb[R:RX, :]).then_inc(xp_stored, 16)
            for j in range(4, 6):
                k_copy(0, j, True)
            for c in range(C):
                ab, lg = w[:, 2 * (c % 2)], w[:, 2 * (c % 2) + 1]
                act.wait_ge(sp_done, 2 * c + 1)
                if c >= 2:
                    act.wait_ge(sp_done, 2 * (c - 1))
                act.activation(ab.rearrange("p (h t) -> p h t", t=HT), misc[:, 2 * (c % 2):2 * (c % 2) + 2], ACT.Abs,
                               bias=dtb[:, c:c + 1]).then_inc(sp_abs, 1)
                act.wait_ge(sp_abs, c + 1)
                act.activation(ab, ab, ACT.Exp, scale=-1.0).then_inc(sp_exp, 1)
                act.wait_ge(sp_exp, c + 1)
                act.activation(lg, ab, ACT.Ln, bias=1.0).then_inc(sp_log, 1)
                if c == 1:
                    for j in range(6, KP):
                        k_copy(0, j, True)
            act.wait_ge(xp_stored, 16)
            for n in range(2):
                load_bc(n, n)
            act.wait_ge(k_done, KP)
            split_w(2, wk_hi)
            for b in range(B):
                v_copy(0, b, True)
            act.wait_ge(a_neg, 1)
            with act.Fori(1, LAST_TRI) as g:
                group(g, all_steps(TRI), TRI)
            group(LAST_TRI, all_steps(TRI), TRI - 1)
            group(LAST_TRI + 1, all_steps(N - TRI * LAST_TRI), 0)
            g = NG - 1
            act.wait_ge(v_done, B * g)
            split_w(2 * g + 1, wv_hi)
            for j in range(5):
                k_copy(g, j)
            inverse_root(2, slice(0, B))
            for j in range(5, KP):
                k_copy(g, j)
            for b in range(2):
                v_copy(g, b)
            inverse_root(3, slice(0, B))
            v_copy(g, 2)

            def split_wq(g, p):
                act.wait_ge(wq_in[p], in_count(g, p, 16))
                if not known(g) or g > 1:
                    act.wait_ge(q_done, g - 1)
                act.activation(wq_hi[p][:], wq_raw[p][:], ACT.Copy).then_inc(wq_hi_done, 1)

            def split_wo(g, p):
                act.wait_ge(wo_in[p], in_count(g, p, 16))
                if not known(g) or g > 1:
                    act.wait_ge(o_done, g - 1)
                act.activation(wo_hi[p][:], wo_raw[p][:], ACT.Copy).then_inc(wo_hi_done, 1)

            def z_split(c):
                act.wait_ge(zt_ps, c + 1)
                act.activation(z_hi[:, c].rearrange("p (h t) -> p h t", t=HT), misc[:, 2 * (c % 2):2 * (c % 2) + 2], ACT.Copy,
                               scale=lnw[:, c:c + 1]).then_inc(z_hi_done, 1)

            for c in range(C):
                z_split(c)
                v_copy(g, 3 + c)
            v_copy(g, 7)
            split_wq(0, 0)

            def step(g, par, half):
                p = par % 2
                if runs(g):
                    act.wait_ge(q_done, g + 1)
                    if not known(g) or g > 1:
                        act.wait_ge(s_done, g - 1)
                    act.activation(q_sb[p][:], psQ, ACT.Copy).then_inc(q_evac, 1)
                if runs(g) and runs(g + 1):
                    split_wq(g + 1, 1 - p)
                if runs(g - 2):
                    split_wo(g - 2, p)
                    act.wait_ge(pv_done, g - 1)
                    if not known(g) or g > 3:
                        act.wait_ge(o_done, g - 3)
                    act.activation(ot_hi[p][:], psO, ACT.Copy).then_inc(ot_hi_done, 1)
                if runs(g - 1):
                    q = 1 - p
                    act.wait_ge(mx_done, g)
                    for b in range(HB):
                        last = act.activation(prob[q][:, b], prob[q][:, b], ACT.Exp, bias=negm[q][:, b:b + 1],
                                              accum_out=psum[q][:, b:b + 1])
                    last.then_inc(exp_done, 1)

            pipeline(act, step)

            inverse_root(4, slice(0, HB))
            for c in range(C):
                act.wait_ge(weff_sum, c + 1)
                act.activation(weff_hi[:, c], ffn_w[:, c], ACT.Copy).then_inc(weff_hi_done, 1)
            for half in range(2):
                for c in range(C):
                    act.wait_ge(zf_ps, C * half + c + 1)
                    act.activation(zf_hi[:, c, half * HT:(half + 1) * HT], misc[:, c], ACT.Copy).then_inc(zf_hi_done, 1)
                if half == 0:
                    inverse_root(5, slice(HB, B))

        @block.vector
        def _(dve):
            links = [0]

            def link(ins):
                links[0] += 1
                ins.then_inc(dve_chain, 1)
                dve.wait_ge(dve_chain, links[0])

            def moments(tile, bs):
                for b in bs:
                    last = dve.bn_stats(stats[:, b], tile[:, b])
                link(last)
                for b in bs:
                    last = dve.bn_aggr(mv[:, b], stats[:, b])
                link(last)

            def refine(n, part):
                dve.wait_ge(ln_exp, n)
                link(dve.tensor_tensor(tmp8[:, part], rstd[:, part], rstd[:, part], ALU.mult))
                link(dve.tensor_tensor(tmp8[:, part], tmp8[:, part], var[:, part], ALU.mult))
                link(dve.tensor_scalar(tmp8[:, part], tmp8[:, part], -0.5, 1.5, ALU.mult, ALU.add))
                link(dve.tensor_tensor(rstd[:, part], rstd[:, part], tmp8[:, part], ALU.mult))

            def norm(out, tile, b):
                return dve.tensor_scalar(out, tile, mv[:, b, 0:1], rstd[:, b:b + 1], ALU.subtract, ALU.mult)

            for c in range(C):
                dve.wait_ge(ctx_hi_done, c + 1)
                dve.tensor_tensor(ctx_lo[:, c], ctx_raw[:, c], ctx_hi[:, c].bitcast(F32), ALU.subtract).then_inc(ctx_lo_done, 1)
            everyone = slice(0, B)
            for i in range(2):
                dve.wait_ge(x_in[i], 16)
                moments(w_tok, range(HB * i, HB * (i + 1)))
            dve.tensor_scalar(var[:], mv[:, :, 1], EPS, None, ALU.add).then_inc(ln_var, 1)
            refine(1, everyone)
            for b in range(B):
                norm(w_tok[:, b], w_tok[:, b], b).then_inc(ln1_done, 1)
            dve.wait_ge(params_in, 16 * 7)
            dve.tensor_scalar(maskadd[:], maskraw[:], 1.0, -MASKED, ALU.subtract, ALU.mult).then_inc(mask_done, 1)
            dve.tensor_reduce(anykey[:], maskraw[:], AX_X, ALU.max).then_inc(mask_done, 1)
            for c in range(C):
                e, lg, v = w[:, 2 * (c % 2)], w[:, 2 * (c % 2) + 1], dA[c % 2][:, :, :].rearrange("p b s -> p (b s)")
                dve.wait_ge(dt_ps, c + 1)
                dve.tensor_scalar(dt_[:, c].rearrange("p (h t) -> p h t", t=HT), misc[:, 2 * (c % 2):2 * (c % 2) + 2],
                                  dtb[:, c:c + 1], 0.0, ALU.add, ALU.max).then_inc(sp_done, 1)
                dve.wait_ge(sp_log, c + 1)
                link(dve.tensor_scalar(v, e, 1.0, -1.0, ALU.add, ALU.add))
                link(dve.tensor_tensor(e, e, v, ALU.subtract))
                link(dve.tensor_tensor(lg, lg, e, ALU.add))
                last = dve.tensor_tensor(dt_[:, c], dt_[:, c], lg, ALU.add)
                last.then_inc(sp_done, 1)
                dve.wait_ge(sp_done, 2 * c + 2)
                link(dve.tensor_tensor(u[:, c], dt_[:, c], y[:, c], ALU.mult))
                dve.tensor_scalar(y[:, c], y[:, c], dskip[:, c:c + 1], None, ALU.mult).then_inc(y_ready, 1)
            for i in range(2):
                dve.memset(dA[i][:, :, 0:1], 0.0).then_inc(da_free, 1)

            def dbx(g, t, c):
                j = J * (g - 1) + C * t + c
                dve.wait_ge(y_ready, j + 1)
                if c == 0:
                    dve.wait_ge(bc_in[t], 16 * g)
                dve.tensor_tensor(w[:, c], u[:, c], bc[t][:, 0], ALU.mult).then_inc(dbx_done, 1)

            def scan_step(g, t, c):
                j = J * (g - 1) + C * t + c
                dve.wait_ge(dbx_done, j + 1)
                dve.wait_ge(da_ready, j + 1)
                dve.tensor_tensor_scan(w[:, c], dA[c % 2][:, :, :].rearrange("p b s -> p (b s)"), w[:, c], 0.0,
                                       ALU.mult, ALU.add).then_inc(da_free, 1)

            def times_c(g, t, c):
                j = J * (g - 1) + C * t + c
                dve.wait_ge(da_free, j + 3)
                dve.tensor_tensor(w[:, c], w[:, c], bc[t][:, 1], ALU.mult).then_inc(prod_done, 1)

            def states(g, count):
                steps = [(g, t, c) for t in range(count) for c in range(C)]
                dbx(*steps[0])
                for i, now in enumerate(steps):
                    if i + 1 < len(steps):
                        dbx(*steps[i + 1])
                    if i:
                        times_c(*steps[i - 1])
                    scan_step(*now)
                times_c(*steps[-1])

            with dve.Fori(1, LAST_TRI + 1) as g:
                states(g, TRI)
            states(LAST_TRI + 1, N - TRI * LAST_TRI)

            dve.wait_ge(x_again, 16)
            for b in range(B):
                dve.wait_ge(yt_ps, b + 1)
                dve.tensor_tensor(base[:, b], base[:, b], misc[:, b % 4], ALU.add).then_inc(x1_done, 1)
            dve.wait_ge(x1_done, B)
            moments(base, range(B))
            dve.tensor_scalar(var[:], mv[:, :, 1], EPS, None, ALU.add).then_inc(ln_var, 1)
            refine(2, everyone)
            for b in range(B):
                last = norm(w_tok[:, b], base[:, b], b)
            link(last)
            moments(w_tok, range(B))
            link(dve.tensor_tensor(tmp8[:], mv[:, :, 0], mv[:, :, 0], ALU.mult))
            link(dve.tensor_tensor(tmp8[:], tmp8[:], mv[:, :, 1], ALU.add))
            dve.tensor_scalar(var[:], tmp8[:], EPS, None, ALU.add).then_inc(ln_var, 1)
            for b in range(B):
                last = dve.tensor_tensor(base[:, b], base[:, b], w_tok[:, b], ALU.add)
            link(last)
            refine(3, everyone)
            for b in range(B):
                dve.tensor_scalar(w_tok[:, b], w_tok[:, b], rstd[:, b:b + 1], None, ALU.mult).then_inc(zn_done, 1)
            for c in range(C):
                dve.wait_ge(z_hi_done, c + 1)
                dve.scalar_tensor_tensor(z_lo[:, c].rearrange("p (h t) -> p h t", t=HT), misc[:, 2 * (c % 2):2 * (c % 2) + 2],
                                         lnw[:, c:c + 1], z_hi[:, c].bitcast(F32).rearrange("p (h t) -> p h t", t=HT),
                                         ALU.mult, ALU.subtract).then_inc(z_lo_done, 1)

            def step(g, par, half):
                p = par % 2
                if runs(g - 2):
                    sh = (g - 2) // H if known(g) else half
                    dve.wait_ge(exp_done, g - 1)
                    dve.reciprocal(rec[p][:], psum[p][:]).then_inc(rec_done, 1)
                    dve.wait_ge(rec_done, g - 1)
                    dve.tensor_tensor(rec[p][:], rec[p][:], anykey[:, sh * HB:(sh + 1) * HB], ALU.mult).then_inc(recv_done, 1)
                    dve.wait_ge(recv_done, g - 1)
                    dve.tensor_tensor(prob[p][:], prob[p][:], rec[p][:, :].unsqueeze(2).to_broadcast([P, HB, S]),
                                      ALU.mult).then_inc(p_ready, 1)
                    dve.wait_ge(t_done, g - 1)
                    if not known(g) or g > 3:
                        dve.wait_ge(pv_done, g - 3)
                    dve.tensor_copy(pt_sb[p][:, :, :].rearrange("p b q -> p (b q)"), psT).then_inc(pt_evac, 1)
                if runs(g - 1):
                    q = 1 - p
                    dve.wait_ge(s_done, g)
                    if not known(g) or g > 2:
                        dve.wait_ge(t_done, g - 2)
                    dve.tensor_tensor(prob[q][:], psS.rearrange("p (b k) -> p b k", k=S),
                                      bias[q][:, :].unsqueeze(1).to_broadcast([P, HB, S]), ALU.add).then_inc(sb_done, 1)
                    dve.wait_ge(sb_done, g)
                    dve.tensor_reduce(negm[q][:], prob[q][:], AX_X, ALU.max, negate=True).then_inc(mx_done, 1)
                if runs(g - 2):
                    dve.wait_ge(ot_hi_done, g - 1)
                    dve.tensor_tensor(ot_lo[p][:], psO, ot_hi[p][:].bitcast(F32), ALU.subtract).then_inc(ot_lo_done, 1)
                if known(g) and g - 3 in (H - 1, STEPS - 1):
                    ended = (g - 3) // H
                    dve.wait_ge(o_done, g - 2)
                    for b in range(HB):
                        dve.tensor_tensor(base[:, ended * HB + b], base[:, ended * HB + b], acc[:, b], ALU.add).then_inc(x2_done, 1)

            def last_norm(half):
                part = slice(half * HB, (half + 1) * HB)
                bs = range(half * HB, (half + 1) * HB)
                dve.wait_ge(x2_done, (half + 1) * HB)
                moments(base, bs)
                dve.tensor_scalar(var[:, part], mv[:, part, 1], EPS, None, ALU.add).then_inc(ln_var, 1)
                refine(4 + half, part)
                for b in bs:
                    norm(xn[:, b], base[:, b], b).then_inc(ln3_done, 1)
                dve.wait_ge(ln3_done, (half + 1) * HB)
                for b in bs:
                    last = dve.tensor_tensor(base[:, b], base[:, b], ffn_b[:], ALU.add)
                link(last)

            def f_split(half):
                for c in range(C):
                    dve.wait_ge(zf_hi_done, C * half + c + 1)
                    dve.tensor_tensor(zf_lo[:, c, half * HT:(half + 1) * HT], misc[:, c],
                                      zf_hi[:, c, half * HT:(half + 1) * HT].bitcast(F32), ALU.subtract).then_inc(zf_lo_done, 1)

            def finish(half):
                for b in range(half * HB, (half + 1) * HB):
                    dve.wait_ge(f_done, b + 1)
                    dve.tensor_tensor(base[:, b], base[:, b], acc[:, b % HB], ALU.add).then_inc(out_ready, 1)

            pipeline(dve, step)
            dve.wait_ge(ffn_in, 16 * 6)
            last_norm(0)
            for c in range(C):
                dve.wait_ge(weff_ps, c + 1)
                dve.tensor_tensor(ffn_w[:, c], ffn_w[:, c], misc[:, c], ALU.add).then_inc(weff_sum, 1)
            for c in range(C):
                dve.wait_ge(weff_hi_done, c + 1)
                dve.tensor_tensor(weff_lo[:, c], ffn_w[:, c], weff_hi[:, c].bitcast(F32), ALU.subtract).then_inc(weff_lo_done, 1)
            f_split(0)
            last_norm(1)
            finish(0)
            f_split(1)
            finish(1)

        @block.gpsimd
        def _(pool):
            for i, m in enumerate((ident, identb)):
                pool.memset(m[:], 0.0).then_inc(ident_set, 1)
                pool.wait_ge(ident_set, i + 1)
                pool.affine_select(out=m[:], in_=m[:], compare_op=ALU.not_equal, fill=1.0, base=0,
                                   pattern=[[-1, P]], channel_multiplier=1).then_inc(ident_done, 1)

            def low_w(m, hi, lo):
                pool.wait_ge(w_hi_done, m + 1)
                pool.tensor_tensor(lo[:], wraw[:], hi[:].bitcast(F32), ALU.subtract).then_inc(w_lo_done, 1)

            def add_y(g, t, c):
                j = J * (g - 1) + C * t + c
                pool.wait_ge(prod_done, j + 1)
                pool.tensor_tensor(y[:, c], y[:, c], w[:, c], ALU.add).then_inc(y_ready, 1)

            def group(g, more_w=True, count=TRI):
                low_w(2 * g + 1, wv_hi, wv_lo)
                steps = [(t, c) for t in range(count) for c in range(C)]
                for t, c in steps[:len(steps) // 2]:
                    add_y(g, t, c)
                if more_w:
                    low_w(2 * g + 2, wk_hi, wk_lo)
                for t, c in steps[len(steps) // 2:]:
                    add_y(g, t, c)

            low_w(0, wk_hi, wk_lo)
            low_w(1, wv_hi, wv_lo)
            low_w(2, wk_hi, wk_lo)
            with pool.Fori(1, LAST_TRI + 1) as g:
                group(g)
            for c in range(C):
                add_y(LAST_TRI + 1, 0, c)
            for m in range(2 * LAST_TRI + 3, 2 * NG):
                low_w(m, *((wv_hi, wv_lo) if m % 2 else (wk_hi, wk_lo)))

            def low_wq(g, p):
                pool.wait_ge(wq_hi_done, g + 1)
                pool.tensor_tensor(wq_lo[p][:], wq_raw[p][:], wq_hi[p][:].bitcast(F32), ALU.subtract).then_inc(wq_lo_done, 1)

            low_wq(0, 0)

            def step(g, par, half):
                p = par % 2
                if runs(g) and runs(g + 1):
                    low_wq(g + 1, 1 - p)
                if runs(g - 2):
                    pool.wait_ge(wo_hi_done, g - 1)
                    pool.tensor_tensor(wo_lo[p][:], wo_raw[p][:], wo_hi[p][:].bitcast(F32), ALU.subtract).then_inc(wo_lo_done, 1)

            pipeline(pool, step)
            pool.wait_ge(ffn_in, 16 * 6)
            for e in range(ER):
                pool.tensor_scalar(eb_sb[:, e], eb_sb[:, e], eprob[:, e:e + 1], 1.0, ALU.mult, ALU.mult).then_inc(eb_done, 1)


def kernel(**inputs):
    import numpy as np
    import concourse.bacc as bacc
    from concourse.bass_utils import run_bass_kernel_spmd as run

    x = np.asarray(inputs["x"])

    def chunks(m):
        m = np.asarray(m)
        return m.reshape(m.shape[0] // P, P, -1).transpose(1, 0, 2)

    def groups(m, heads):
        m = np.asarray(m)
        return m.reshape(H // heads, heads * P, C, P).transpose(0, 3, 2, 1)

    arrays = {
        "x": x,
        "ctxT": chunks(np.asarray(inputs["ctx_4096"]).reshape(T, D).T),
        "mask": inputs["mask_BxSxS2_bk0"],
        "A_log": chunks(inputs["L0_attn_A_log"]),
        "D": np.asarray(inputs["L0_attn_D"]).reshape(C, P).T,
        "dt_b": np.asarray(inputs["L0_attn_dt_proj_b"]).reshape(C, P).T,
        "xp_w": chunks(np.asarray(inputs["L0_attn_x_proj_w"]).T),
        "dt_w": np.asarray(inputs["L0_attn_dt_proj_w"]).T,
        "ln_w": np.asarray(inputs["L0_xattn_ln_weight"]).reshape(C, P).T,
        "pbias": inputs["L0_xattn_position_bias"],
        "wq": groups(inputs["L0_xattn_w_q"], 1),
        "wk": groups(inputs["L0_xattn_w_k"], G),
        "wv": groups(inputs["L0_xattn_w_v"], G),
        "wo": np.asarray(inputs["L0_xattn_w_out"]).T.reshape(H, P, D),
        "ffn_w": chunks(np.asarray(inputs["L0_ffn_W"]).T),
        "ffn_a": chunks(np.asarray(inputs["L0_ffn_A"]).reshape(-1, D)),
        "ffn_bw": chunks(np.asarray(inputs["L0_ffn_B"]).transpose(0, 2, 1).reshape(-1, D)),
        "ffn_b": inputs["L0_ffn_b"],
        "probs": np.repeat(np.asarray(inputs["L0_ffn_probs"]), P * ER // E).reshape(-1, 1),
    }
    nc = bacc.Bacc("TRN2", target_bir_lowering=False, num_devices=1)
    a, given = {}, {}
    for name, v in arrays.items():
        v = np.ascontiguousarray(v)
        given[f"in_{name}"] = v
        a[name] = nc.dram_tensor(f"in_{name}", v.shape, mybir.dt.from_np(v.dtype), kind="ExternalInput").ap()
    a["out"] = nc.dram_tensor("out_x", x.shape, F32, kind="ExternalOutput").ap()
    decoder_layer(nc, a)
    r = run(nc, [given], core_ids=[0])
    return r.results[0]["out_x"]
```

```python
from contextlib import ExitStack

import concourse.bass as bass
from concourse import mybir

F32 = mybir.dt.float32
F32R = mybir.dt.float32r
BF16 = mybir.dt.bfloat16
U8 = mybir.dt.uint8
ALU = mybir.AluOpType
ACT = mybir.ActivationFunctionType
AX_X = mybir.AxisListType.X

P = 128
B = 8
S = 128
D = 512
C = D // P
T = B * S
H = 32
N = 16
R = 16
RX = R + 2 * N
G = 4
NG = H // G
HB = B // 2
HT = HB * S
KP = 2 * G
STEPS = 2 * H
TRI = 3
SCANS = (N - 1) // TRI
J = TRI * C
E = 16
ER = E * 16 // P
EPS = 1e-5
MASKED = -1e30


def decoder_layer(nc, a):
    k_dram = nc.dram_tensor("k_scratch", (STEPS, P, HT), F32, kind="Internal").ap()
    v_dram = nc.dram_tensor("v_scratch", (STEPS, P, HT), F32, kind="Internal").ap()
    xp_dram = nc.dram_tensor("xp_scratch", (2, N, T), F32, kind="Internal").ap()
    v_dram_g = v_dram.rearrange("(q h) p x -> q p h x", h=G)

    with ExitStack() as whole:
        def sb(stack, name, shape, dt=F32, side="left"):
            return stack.enter_context(nc.sbuf_tensor(name, shape, dt, side=side))

        acc = whole.enter_context(nc.psum_tensor("acc", [P, 4, 512], F32))
        misc = whole.enter_context(nc.psum_tensor("misc", [P, 4, 512], F32))
        psQ, psS, psT, psO = (misc[:, i, :] for i in range(4))

        base = sb(whole, "base", [P, B, D])
        ident = sb(whole, "ident", [P, P])
        maskadd = sb(whole, "maskadd", [P, B, S], BF16)
        anykey = sb(whole, "anykey", [P, B])
        lnw = sb(whole, "lnw", [P, C])
        stats = sb(whole, "stats", [P, B, 6])
        mv = sb(whole, "mv", [P, B, 2])
        var = sb(whole, "var", [P, B])
        rstd = sb(whole, "rstd", [P, B])
        tmp8 = sb(whole, "tmp8", [P, B])

        with ExitStack() as low:
            ctx_hi = sb(low, "ctx_hi", [P, C, T], F32R, "right")
            ctx_lo = sb(low, "ctx_lo", [P, C, T], F32R, "right")
            wraw = sb(low, "wraw", [P, C, G * P], F32, "right")
            wk_hi = sb(low, "wk_hi", [P, C, G * P], F32R, "right")
            wk_lo = sb(low, "wk_lo", [P, C, G * P], F32R, "right")
            wv_hi = sb(low, "wv_hi", [P, C, G * P], F32R, "right")
            wv_lo = sb(low, "wv_lo", [P, C, G * P], F32R, "right")
            kst = [sb(low, f"kst{i}", [P, HT], F32, "right") for i in range(2)]
            vst = [sb(low, f"vst{i}", [P, G, 2, P], F32, "right") for i in range(2)]

        with ExitStack() as tail:
            zf_hi = sb(tail, "zf_hi", [P, C, T], F32R, "right")
            zf_lo = sb(tail, "zf_lo", [P, C, T], F32R, "right")
            ffn_w = sb(tail, "ffn_w", [P, C, D], F32, "right")
            weff_hi = sb(tail, "weff_hi", [P, C, D], F32R, "right")
            weff_lo = sb(tail, "weff_lo", [P, C, D], F32R, "right")
            ea_sb = sb(tail, "ea_sb", [P, ER, D], F32, "right")
            eb_sb = sb(tail, "eb_sb", [P, ER, D], F32, "right")
            eprob = sb(tail, "eprob", [P, ER], F32, "right")
            ffn_b = sb(tail, "ffn_b", [P, D], F32, "right")
            xn = sb(tail, "xn", [P, B, D], F32, "right")

        with ExitStack() as scan:
            dt_ = sb(scan, "dt_", [P, C, T])
            u = sb(scan, "u", [P, C, T])
            bc = [sb(scan, f"bc{i}", [P, 2, T]) for i in range(TRI)]
            dA = [sb(scan, f"dA{i}", [P, B, S]) for i in range(2)]
            y = sb(scan, "y", [P, C, T])
            w = sb(scan, "w", [P, C, T])
            negA = sb(scan, "negA", [P, C, N])
            dskip = sb(scan, "dskip", [P, C])
            dtb = sb(scan, "dtb", [P, C])
            xpw = sb(scan, "xpw", [P, C, RX])
            dtw = sb(scan, "dtw", [R, D])
            maskraw = sb(scan, "maskraw", [P, B, S], U8)

        pair = range(2)
        z_hi = sb(whole, "z_hi", [P, C, T], F32R)
        z_lo = sb(whole, "z_lo", [P, C, T], F32R)
        wq_raw = [sb(whole, f"wq_raw{i}", [P, C, P]) for i in pair]
        wq_hi = [sb(whole, f"wq_hi{i}", [P, C, P], F32R) for i in pair]
        wq_lo = [sb(whole, f"wq_lo{i}", [P, C, P], F32R) for i in pair]
        wo_raw = [sb(whole, f"wo_raw{i}", [P, D]) for i in pair]
        wo_hi = [sb(whole, f"wo_hi{i}", [P, D], F32R) for i in pair]
        wo_lo = [sb(whole, f"wo_lo{i}", [P, D], F32R) for i in pair]
        k_sb = [sb(whole, f"k_sb{i}", [P, HT]) for i in pair]
        v_sb = [sb(whole, f"v_sb{i}", [P, HB, P]) for i in pair]
        q_sb = [sb(whole, f"q_sb{i}", [P, HT]) for i in pair]
        prob = [sb(whole, f"prob{i}", [P, HB, S]) for i in pair]
        pt_sb = [sb(whole, f"pt_sb{i}", [P, HB, S]) for i in pair]
        bias = [sb(whole, f"bias{i}", [P, S]) for i in pair]
        bm = [sb(whole, f"bm{i}", [P, HB, S]) for i in pair]
        negm = [sb(whole, f"negm{i}", [P, HB]) for i in pair]
        psum = [sb(whole, f"psum{i}", [P, HB]) for i in pair]
        rec = [sb(whole, f"rec{i}", [P, HB]) for i in pair]
        ot_hi = [sb(whole, f"ot_hi{i}", [P, HT], F32R) for i in pair]
        ot_lo = [sb(whole, f"ot_lo{i}", [P, HT], F32R) for i in pair]

        w_tok = w[:, :, :].rearrange("p c (h d) -> p (c h) d", d=D)
        xp_sb = base[:, 0:2, :].rearrange("p h t -> p (h t)")
        ctx_raw = base[:, :, :].rearrange("p (c h) t -> p c (h t)", c=C)

        def sem(name):
            return whole.enter_context(nc.semaphore(name))

        x_in = [sem(f"x_in{i}") for i in range(2)]
        ctx_in = [sem(f"ctx_in{i}") for i in range(C)]
        params_in, x_again, wraw_in = sem("params_in"), sem("x_again"), sem("wraw_in")
        k_stored = [sem(f"k_stored{i}") for i in range(2)]
        v_stored = [sem(f"v_stored{i}") for i in range(2)]
        xp_stored = sem("xp_stored")
        bc_in = [sem(f"bc_in{i}") for i in range(TRI)]
        wq_in = [sem(f"wq_in{i}") for i in pair]
        wo_in = [sem(f"wo_in{i}") for i in pair]
        kb_in = [sem(f"kb_in{i}") for i in pair]
        v_in = [sem(f"v_in{i}") for i in pair]
        ffn_in, out_stored = sem("ffn_in"), sem("out_stored")
        ident_set, ident_done, mask_done = sem("ident_set"), sem("ident_done"), sem("mask_done")
        ctx_hi_done, ctx_lo_done = sem("ctx_hi_done"), sem("ctx_lo_done")
        w_hi_done, w_lo_done = sem("w_hi_done"), sem("w_lo_done")
        k_done, k_evac, v_done, v_evac = sem("k_done"), sem("k_evac"), sem("v_done"), sem("v_evac")
        ln_var, ln_log, ln_exp = sem("ln_var"), sem("ln_log"), sem("ln_exp")
        ln1_done = sem("ln1_done")
        xt_ps, xt_evac, xp_ps, xp_evac, dt_ps = sem("xt_ps"), sem("xt_evac"), sem("xp_ps"), sem("xp_evac"), sem("dt_ps")
        sp_max, sp_abs, sp_exp, sp_log, sp_done = (sem(n) for n in ("sp_max", "sp_abs", "sp_exp", "sp_log", "sp_done"))
        a_exp, a_neg = sem("a_exp"), sem("a_neg")
        y_ready, da_free, da_ready = sem("y_ready"), sem("da_free"), sem("da_ready")
        dbx_done, prod_done = sem("dbx_done"), sem("prod_done")
        yt_ps, x1_done, zn_done, zt_ps = sem("yt_ps"), sem("x1_done"), sem("zn_done"), sem("zt_ps")
        z_hi_done, z_lo_done = sem("z_hi_done"), sem("z_lo_done")
        wq_hi_done, wq_lo_done = sem("wq_hi_done"), sem("wq_lo_done")
        wo_hi_done, wo_lo_done = sem("wo_hi_done"), sem("wo_lo_done")
        q_done, q_evac, s_done, sb_done = sem("q_done"), sem("q_evac"), sem("s_done"), sem("sb_done")
        bm_done = sem("bm_done")
        mx_done, exp_done, rec_done, recv_done = sem("mx_done"), sem("exp_done"), sem("rec_done"), sem("recv_done")
        p_ready, t_done, pt_evac, pv_done = sem("p_ready"), sem("t_done"), sem("pt_evac"), sem("pv_done")
        ot_hi_done, ot_lo_done, o_done, x2_done = sem("ot_hi_done"), sem("ot_lo_done"), sem("o_done"), sem("x2_done")
        eb_done, weff_ps, weff_sum = sem("eb_done"), sem("weff_ps"), sem("weff_sum")
        weff_hi_done, weff_lo_done = sem("weff_hi_done"), sem("weff_lo_done")
        ln3_done, zf_ps = sem("ln3_done"), sem("zf_ps")
        zf_hi_done, zf_lo_done, f_done, out_ready = sem("zf_hi_done"), sem("zf_lo_done"), sem("f_done"), sem("out_ready")
        dve_chain = sem("dve_chain")

        block = whole.enter_context(nc.Block())

        def pipeline(eng, step):
            for g in range(4):
                step(g, g, 0)
            with eng.Fori(2, H // 2 - 1) as i:
                for p in pair:
                    step(2 * i + p, p, 0)
            for g in range(H - 2, H + 4):
                step(g, g, g // H)
            with eng.Fori(H // 2 + 2, H - 1) as i:
                for p in pair:
                    step(2 * i + p, p, 1)
            for g in range(STEPS - 2, STEPS + 3):
                step(g, g, 1)

        def known(g):
            return isinstance(g, int)

        def runs(g):
            return not known(g) or 0 <= g < STEPS

        def in_count(g, p, n):
            return n * (g // 2 + 1) if known(g) else n // 2 * (g - p) + n

        @block.sync
        def _(sp):
            for c in range(C):
                sp.dma_start(wraw[:, c], a["wk"][0][:, c]).then_inc(ctx_in[c], 16)
                sp.dma_start(ctx_raw[:, c], a["ctxT"][:, c]).then_inc(ctx_in[c], 16)
            for i in range(2):
                sp.dma_start(w_tok[:, HB * i:HB * (i + 1)],
                             a["x"][HB * i:HB * (i + 1)].rearrange("b t d -> t b d")).then_inc(x_in[i], 16)
            for dst, src in ((negA, "A_log"), (dskip, "D"), (dtb, "dt_b"), (xpw, "xp_w"), (dtw, "dt_w"), (lnw, "ln_w")):
                sp.dma_start(dst[:], a[src]).then_inc(params_in, 16)
            sp.dma_start(maskraw[:], a["mask"].rearrange("b q k -> q b k")).then_inc(params_in, 16)

            def k_store(g, j):
                sp.wait_ge(k_evac, KP * g + j + 1)
                sp.dma_start(k_dram[H * (j % 2) + G * g + j // 2], kst[j % 2][:]).then_inc(k_stored[j % 2], 16)

            def v_store(g, q):
                sp.wait_ge(v_evac, B * g + 2 * q + 2)
                sp.dma_start(v_dram_g[NG * (q // 2) + g, :, :, 2 * P * (q % 2):2 * P * (q % 2 + 1)],
                             vst[q % 2][:, :, :, :].rearrange("p h b d -> p h (b d)")).then_inc(v_stored[q % 2], 16)

            def k_group(g, more):
                for j in range(KP):
                    k_store(g, j)
                    if more and j == 2:
                        sp.wait_ge(w_lo_done, 2 * g + 1)
                        sp.dma_start(wraw[:], a["wk"][g + 1]).then_inc(wraw_in, 16)

            def v_group(g, more):
                for q in range(4):
                    v_store(g, q)
                    if more and q == 1:
                        sp.wait_ge(w_lo_done, 2 * g + 2)
                        sp.dma_start(wraw[:], a["wv"][g + 1]).then_inc(wraw_in, 16)

            sp.wait_ge(ctx_lo_done, C)
            sp.dma_start(wraw[:], a["wv"][0]).then_inc(wraw_in, 16)
            k_group(0, True)
            v_group(0, True)
            sp.wait_ge(dt_ps, C)
            sp.wait_ge(xp_stored, 16)
            sp.dma_start(base[:], a["x"].rearrange("b t d -> t b d")).then_inc(x_again, 16)
            with sp.Fori(1, SCANS + 1) as g:
                k_group(g, True)
                v_group(g, True)

            def load_wq(h, p):
                sp.dma_start(wq_raw[p][:], a["wq"][h]).then_inc(wq_in[p], 16)

            def load_kb(g, h, p):
                sp.dma_start(k_sb[p][:], k_dram[g]).then_inc(kb_in[p], 16)
                sp.dma_start(bias[p][:], a["pbias"][h]).then_inc(kb_in[p], 16)

            k_group(NG - 2, True)
            sp.wait_ge(prod_done, C * N)
            for g in range(2):
                load_wq(g, g)
            v_group(NG - 2, True)
            k_group(NG - 1, False)
            v_group(NG - 1, False)
            for i in range(2):
                sp.wait_ge(k_stored[i], 16 * KP // 2 * NG)
                sp.wait_ge(v_stored[i], 16 * 2 * NG)
            sp.wait_ge(yt_ps, B)
            load_kb(0, 0, 0)
            sp.wait_ge(v_done, B * NG)
            sp.dma_start(ffn_w[:], a["ffn_w"]).then_inc(ffn_in, 16)
            sp.dma_start(ea_sb[:], a["ffn_a"]).then_inc(ffn_in, 16)
            sp.dma_start(eb_sb[:], a["ffn_bw"]).then_inc(ffn_in, 16)
            sp.dma_start(ffn_b[:], a["ffn_b"].partition_broadcast(P)).then_inc(ffn_in, 16)
            for e in range(ER):
                sp.dma_start(eprob[:, e:e + 1], a["probs"][P * e:P * (e + 1), :]).then_inc(ffn_in, 16)

            def head(g, half):
                return g % H if known(g) else g - H * half

            def step(g, par, half):
                p = par % 2
                if runs(g) and runs(g + 2):
                    sp.wait_ge(wq_lo_done, g + 1)
                    load_wq(head(g + 2, half), p)
                if runs(g) and runs(g + 1):
                    if not known(g) or g >= 1:
                        sp.wait_ge(sb_done, g)
                    load_kb(g + 1, head(g + 1, half), 1 - p)
                if runs(g):
                    if not known(g) or g >= 2:
                        sp.wait_ge(pv_done, g - 1)
                    sp.dma_start(v_sb[p][:, :, :].rearrange("p b d -> p (b d)"), v_dram[g]).then_inc(v_in[p], 16)
                    if not known(g) or g >= 2:
                        sp.wait_ge(wo_lo_done, g - 1)
                    sp.dma_start(wo_raw[p][:], a["wo"][head(g, half)]).then_inc(wo_in[p], 16)

            pipeline(sp, step)
            for b in range(B):
                sp.wait_ge(out_ready, b + 1)
                sp.dma_start(a["out"][b], base[:, b]).then_inc(out_stored, 16)
            sp.wait_ge(out_stored, 16 * B)

        @block.tensor
        def _(pe):
            def three(out, w_hi, w_lo, m_hi, m_lo, first, last):
                pe.matmul(out, w_hi, m_hi, start=first, stop=False)
                pe.matmul(out, w_hi, m_lo, start=False, stop=False)
                return pe.matmul(out, w_lo, m_hi, start=False, stop=last)

            def k_part(j, bank, c):
                hd, half = slice(j // 2 * P, (j // 2 + 1) * P), slice(j % 2 * HT, (j % 2 + 1) * HT)
                return three(acc[:, bank], wk_hi[:, c, hd], wk_lo[:, c, hd], ctx_hi[:, c, half], ctx_lo[:, c, half],
                             c == 0, c == C - 1)

            def k_sum(g, j):
                pe.wait_ge(k_evac, KP * g + j - 1)
                for c in range(C):
                    mm = k_part(j, j % 2, c)
                mm.then_inc(k_done, 1)

            def v_sum(g, b, first=False):
                if not first or b >= 2:
                    pe.wait_ge(v_evac, B * g + b - 1)
                tok = slice(b * S, (b + 1) * S)
                for c in range(C):
                    mm = three(acc[:, 2 + b % 2], ctx_hi[:, c, tok], ctx_lo[:, c, tok], wv_hi[:, c], wv_lo[:, c],
                               c == 0, c == C - 1)
                mm.then_inc(v_done, 1)

            for c in range(C):
                pe.wait_ge(ctx_lo_done, c + 1)
                for j in range(4):
                    mm = k_part(j, j, c)
                    if c == C - 1:
                        mm.then_inc(k_done, 1)

            def k_sum_0(j):
                pe.wait_ge(k_evac, j - 3 if j < 6 else j - 1)
                for c in range(C):
                    mm = k_part(j, j % 2, c)
                mm.then_inc(k_done, 1)

            def dt_proj(c):
                if c >= 2:
                    pe.wait_ge(sp_abs, c - 1)
                for half in range(2):
                    mm = pe.matmul(misc[:, 2 * (c % 2) + half], dtw[:, c * P:(c + 1) * P],
                                   xp_sb[0:R, half * HT:(half + 1) * HT], start=True, stop=True)
                mm.then_inc(dt_ps, 1)

            for j in range(4, 7):
                k_sum_0(j)
            pe.wait_ge(ident_done, 1)
            for c in range(C):
                if c >= 2:
                    pe.wait_ge(xt_evac, c - 1)
                for b in range(B):
                    if c == 0:
                        pe.wait_ge(ln1_done, b + 1)
                    mm = pe.transpose(misc[:, 2 * (c % 2) + b // HB, b % HB * S:(b % HB + 1) * S],
                                      w_tok[:, b, c * P:(c + 1) * P], ident[:])
                mm.then_inc(xt_ps, 1)
            k_sum_0(7)
            pe.wait_ge(params_in, 16 * 7)
            pe.wait_ge(xt_evac, C)
            for half in range(2):
                for c in range(C):
                    mm = pe.matmul(misc[0:RX, half], xpw[:, c], y[:, c, half * HT:(half + 1) * HT],
                                   start=(c == 0), stop=(c == C - 1))
            mm.then_inc(xp_ps, 1)
            pe.wait_ge(w_lo_done, 1)
            v_sum(0, 0, True)
            pe.wait_ge(xp_evac, 1)
            for c in range(2):
                dt_proj(c)
            v_sum(0, 1, True)
            for c in range(2, C):
                dt_proj(c)
            for b in range(2, B):
                v_sum(0, b, True)

            def k_group(g, js):
                pe.wait_ge(w_lo_done, 2 * g)
                for j in js:
                    k_sum(g, j)

            def v_group(g):
                pe.wait_ge(w_lo_done, 2 * g + 1)
                for b in range(B):
                    v_sum(g, b)

            with pe.Fori(1, SCANS + 1) as g:
                k_group(g, range(KP))
                v_group(g)

            k_group(NG - 2, range(KP))
            pe.wait_ge(y_ready, C * N + C)
            for b in range(B):
                if b >= 4:
                    pe.wait_ge(x1_done, b - 3)
                for c in range(C):
                    mm = pe.transpose(misc[:, b % 4, c * P:(c + 1) * P], y[:, c, b * S:(b + 1) * S], ident[:])
                mm.then_inc(yt_ps, 1)
            v_group(NG - 2)
            k_group(NG - 1, range(4))
            for c in range(C):
                if c >= 2:
                    pe.wait_ge(z_lo_done, c - 1)
                for b in range(B):
                    if c == 0:
                        pe.wait_ge(zn_done, b + 1)
                    mm = pe.transpose(misc[:, 2 * (c % 2) + b // HB, b % HB * S:(b % HB + 1) * S],
                                      w_tok[:, b, c * P:(c + 1) * P], ident[:])
                mm.then_inc(zt_ps, 1)
                k_sum(NG - 1, 4 + c)
            v_group(NG - 1)
            pe.wait_ge(z_lo_done, C)

            def weff_sum_of(c):
                if c == 0:
                    pe.wait_ge(eb_done, ER)
                    pe.wait_ge(q_evac, STEPS)
                else:
                    pe.wait_ge(weff_sum, c)
                for e in range(ER):
                    mm = pe.matmul(psQ, ea_sb[:, e, c * P:(c + 1) * P], eb_sb[:, e], start=(e == 0), stop=(e == ER - 1))
                mm.then_inc(weff_ps, 1)

            def f_input(half, *free):
                bank = acc if half else misc
                for c in range(C):
                    pe.wait_ge(*free[c])
                    for b in range(HB):
                        if c == 0:
                            pe.wait_ge(ln3_done, half * HB + b + 1)
                        mm = pe.transpose(bank[:, c, b * S:(b + 1) * S], xn[:, half * HB + b, c * P:(c + 1) * P], ident[:])
                    mm.then_inc(zf_ps, 1)

            def step(g, par, half):
                p = par % 2
                if known(g) and STEPS <= g <= STEPS + 1:
                    weff_sum_of(2 * (g - STEPS))
                if known(g) and g == STEPS + 2:
                    f_input(0, (weff_sum, C), (sb_done, STEPS), (pt_evac, STEPS), (ot_lo_done, STEPS))
                if runs(g):
                    tok = slice(half * HT, (half + 1) * HT)
                    pe.wait_ge(wq_lo_done, g + 1)
                    if not known(g) or g:
                        pe.wait_ge(q_evac, g)
                    for c in range(C):
                        mm = three(psQ, wq_hi[p][:, c], wq_lo[p][:, c], z_hi[:, c, tok], z_lo[:, c, tok],
                                   c == 0, c == C - 1)
                    mm.then_inc(q_done, 1)
                if runs(g - 2):
                    pe.wait_ge(p_ready, g - 1)
                    if not known(g) or g > 2:
                        pe.wait_ge(pt_evac, g - 2)
                    for b in range(HB):
                        mm = pe.transpose(psT[:, b * S:(b + 1) * S], prob[p][:, b], ident[:])
                    mm.then_inc(t_done, 1)
                if runs(g - 1):
                    pe.wait_ge(q_evac, g)
                    pe.wait_ge(kb_in[1 - p], in_count(g - 1, 1 - p, 32))
                    if not known(g) or g > 1:
                        pe.wait_ge(sb_done, g - 1)
                    for b in range(HB):
                        mm = pe.matmul(psS[:, b * S:(b + 1) * S], q_sb[1 - p][:, b * S:(b + 1) * S],
                                       k_sb[1 - p][:, b * S:(b + 1) * S], start=True, stop=True)
                    mm.then_inc(s_done, 1)
                if runs(g - 2):
                    pe.wait_ge(pt_evac, g - 1)
                    pe.wait_ge(v_in[p], in_count(g - 2, p, 16))
                    if not known(g) or g > 2:
                        pe.wait_ge(ot_lo_done, g - 2)
                    for b in range(HB):
                        mm = pe.matmul(psO[:, b * S:(b + 1) * S], v_sb[p][:, b], pt_sb[p][:, b], start=True, stop=True)
                    mm.then_inc(pv_done, 1)
                if known(g) and STEPS <= g <= STEPS + 1:
                    weff_sum_of(2 * (g - STEPS) + 1)
                if runs(g - 3):
                    h = (g - 3) % H if known(g) else 1
                    q = 1 - p
                    if known(g) and g == 3:
                        pe.wait_ge(k_evac, KP * NG)
                        pe.wait_ge(v_evac, B * NG)
                    pe.wait_ge(ot_lo_done, g - 2)
                    pe.wait_ge(wo_lo_done, g - 2)
                    for b in range(HB):
                        tok = slice(b * S, (b + 1) * S)
                        if known(g) and g - 3 == H:
                            pe.wait_ge(x2_done, b + 1)
                        mm = three(acc[:, b], ot_hi[q][:, tok], ot_lo[q][:, tok], wo_hi[q][:], wo_lo[q][:],
                                   h == 0, h == H - 1)
                    mm.then_inc(o_done, 1)

            pipeline(pe, step)

            pe.wait_ge(weff_lo_done, C)
            for half in range(2):
                if half:
                    f_input(1, *((x2_done, HB + c + 1) for c in range(C)))
                for b in range(half * HB, (half + 1) * HB):
                    if half:
                        pe.wait_ge(out_ready, b - HB + 1)
                    tok = slice(b * S, (b + 1) * S)
                    for c in range(C):
                        if b == half * HB:
                            pe.wait_ge(zf_lo_done, C + c + 1 if half else C)
                        mm = three(misc[:, b % HB], zf_hi[:, c, tok], zf_lo[:, c, tok], weff_hi[:, c], weff_lo[:, c],
                                   c == 0, c == C - 1)
                    mm.then_inc(f_done, 1)

        @block.scalar
        def _(act):
            def inverse_root(n, part):
                act.wait_ge(ln_var, n)
                act.activation(tmp8[:, part], var[:, part], ACT.Ln).then_inc(ln_log, 1)
                act.wait_ge(ln_log, n)
                act.activation(rstd[:, part], tmp8[:, part], ACT.Exp, scale=-0.5).then_inc(ln_exp, 1)

            def split_w(m, hi):
                act.wait_ge(wraw_in, 16 * m)
                act.activation(hi[:], wraw[:], ACT.Copy).then_inc(w_hi_done, 1)

            def k_copy(g, j, first=False):
                act.wait_ge(k_done, KP * g + j + 1)
                if not first or j >= 2:
                    act.wait_ge(k_stored[j % 2], 16 * (KP // 2 * g + j // 2))
                bank = j if first and j < 4 else j % 2
                act.activation(kst[j % 2][:], acc[:, bank], ACT.Copy).then_inc(k_evac, 1)

            def v_copy(g, b, first=False):
                act.wait_ge(v_done, B * g + b + 1)
                q = b // 2
                if not first or q >= 2:
                    act.wait_ge(v_stored[q % 2], 16 * (2 * g + q // 2))
                act.activation(vst[q % 2][:, :, b % 2], acc[:, 2 + b % 2].rearrange("p (h d) -> p h d", d=P),
                               ACT.Copy).then_inc(v_evac, 1)

            def dA_exp(g, t, c):
                n = TRI * (g - 1) + 1 + t
                act.wait_ge(da_free, J * (g - 1) + C * (t + 1) + c + 1)
                act.activation(dA[c % 2][:, :, 1:S], dt_[:, c].rearrange("p (b s) -> p b s", s=S)[:, :, 1:S],
                               ACT.Exp, scale=negA[:, c, bass.ds(n, 1)]).then_inc(da_ready, 1)

            def load_bc(n, i):
                act.dma_start(bc[i][:], xp_dram[:, n].partition_broadcast(P)).then_inc(bc_in[i], 16)

            def state_exp(g, t, c, bc_loads):
                dA_exp(g, t, c)
                if c == C - 1 and t < bc_loads:
                    load_bc(TRI * g + t, t)

            steps = [(t, c) for t in range(TRI) for c in range(C)]

            def group(g, bc_loads):
                act.wait_ge(v_done, B * g)
                split_w(2 * g + 1, wv_hi)
                copies = [(k_copy, j) for j in range(KP)] + [(v_copy, b) for b in range(B)]
                left = list(steps)
                for i, (copy, j) in enumerate(copies):
                    if i == KP:
                        act.wait_ge(k_done, KP * g + KP)
                        split_w(2 * g + 2, wk_hi)
                    if i % 4 != 3:
                        state_exp(g, *left.pop(0), bc_loads)
                    copy(g, j)

            for c in range(C):
                act.wait_ge(ctx_in[c], 32)
                act.activation(wk_hi[:, c], wraw[:, c], ACT.Copy)
                act.activation(ctx_hi[:, c], ctx_raw[:, c], ACT.Copy).then_inc(ctx_hi_done, 1)
            for j in range(2):
                k_copy(0, j, True)
            inverse_root(1, slice(0, B))
            split_w(1, wv_hi)
            for j in range(2, 7):
                k_copy(0, j, True)
            for c in range(C):
                act.wait_ge(xt_ps, c + 1)
                act.activation(y[:, c].rearrange("p (h t) -> p h t", t=HT), misc[:, 2 * (c % 2):2 * (c % 2) + 2],
                               ACT.Copy).then_inc(xt_evac, 1)
            k_copy(0, 7, True)
            act.wait_ge(params_in, 16 * 7)
            act.activation(negA[:], negA[:], ACT.Exp).then_inc(a_exp, 1)
            act.wait_ge(a_exp, 1)
            act.activation(negA[:], negA[:], ACT.Copy, scale=-1.0).then_inc(a_neg, 1)
            act.wait_ge(xp_ps, 1)
            act.activation(xp_sb[0:RX, :].rearrange("p (h t) -> p h t", t=HT), misc[0:RX, 0:2], ACT.Copy).then_inc(xp_evac, 1)
            act.wait_ge(xp_evac, 1)
            act.dma_start(xp_dram.rearrange("a n t -> (a n) t"), xp_sb[R:RX, :]).then_inc(xp_stored, 16)
            v_copy(0, 0, True)

            def softplus_parts(c):
                act.wait_ge(sp_max, c + 1)
                act.activation(w[:, c].rearrange("p (h t) -> p h t", t=HT), misc[:, 2 * (c % 2):2 * (c % 2) + 2], ACT.Abs,
                               bias=dtb[:, c:c + 1]).then_inc(sp_abs, 1)
                act.wait_ge(sp_abs, c + 1)
                act.activation(w[:, c], w[:, c], ACT.Exp, scale=-1.0).then_inc(sp_exp, 1)
                act.wait_ge(sp_exp, c + 1)
                act.activation(u[:, c], w[:, c], ACT.Ln, bias=1.0).then_inc(sp_log, 1)

            for c in range(2):
                softplus_parts(c)
            v_copy(0, 1, True)
            act.wait_ge(xp_stored, 16)
            for n in range(2):
                act.dma_start(bc[n][:], xp_dram[:, n].partition_broadcast(P)).then_inc(bc_in[n], 16)
            for c in range(2, C):
                softplus_parts(c)
            v_copy(0, 2, True)
            act.wait_ge(k_done, KP)
            split_w(2, wk_hi)
            act.wait_ge(a_neg, 1)
            v_copy(0, 3, True)
            for c in range(C):
                state_exp(0, TRI - 1, c, TRI)
                v_copy(0, 4 + c, True)
            with act.Fori(1, SCANS) as g:
                group(g, TRI)
            group(SCANS, 1)
            g = NG - 2
            act.wait_ge(v_done, B * g)
            split_w(2 * g + 1, wv_hi)
            for j in range(KP):
                k_copy(g, j)
            act.wait_ge(k_done, KP * g + KP)
            split_w(2 * g + 2, wk_hi)
            for b in range(3):
                v_copy(g, b)
            inverse_root(2, slice(0, B))
            for b in range(3, B):
                v_copy(g, b)
            inverse_root(3, slice(0, B))
            g = NG - 1
            act.wait_ge(v_done, B * g)
            split_w(2 * g + 1, wv_hi)
            for j in range(4):
                k_copy(g, j)

            def split_wq(g, p):
                act.wait_ge(wq_in[p], in_count(g, p, 16))
                if not known(g) or g > 1:
                    act.wait_ge(q_done, g - 1)
                act.activation(wq_hi[p][:], wq_raw[p][:], ACT.Copy).then_inc(wq_hi_done, 1)

            def split_wo(g, p):
                act.wait_ge(wo_in[p], in_count(g, p, 16))
                if not known(g) or g > 1:
                    act.wait_ge(o_done, g - 1)
                act.activation(wo_hi[p][:], wo_raw[p][:], ACT.Copy).then_inc(wo_hi_done, 1)

            def z_split(c):
                act.wait_ge(zt_ps, c + 1)
                act.activation(z_hi[:, c].rearrange("p (h t) -> p h t", t=HT), misc[:, 2 * (c % 2):2 * (c % 2) + 2], ACT.Copy,
                               scale=lnw[:, c:c + 1]).then_inc(z_hi_done, 1)

            for c in range(C):
                z_split(c)
                k_copy(g, 4 + c)
            split_wq(0, 0)
            for b in range(B):
                v_copy(g, b)

            def step(g, par, half):
                p = par % 2
                if runs(g):
                    act.wait_ge(q_done, g + 1)
                    if not known(g) or g > 1:
                        act.wait_ge(s_done, g - 1)
                    act.activation(q_sb[p][:], psQ, ACT.Copy).then_inc(q_evac, 1)
                if runs(g) and runs(g + 1):
                    split_wq(g + 1, 1 - p)
                if runs(g - 2):
                    split_wo(g - 2, p)
                    act.wait_ge(pv_done, g - 1)
                    if not known(g) or g > 3:
                        act.wait_ge(o_done, g - 3)
                    act.activation(ot_hi[p][:], psO, ACT.Copy).then_inc(ot_hi_done, 1)
                if runs(g - 1):
                    q = 1 - p
                    act.wait_ge(mx_done, g)
                    for b in range(HB):
                        last = act.activation(prob[q][:, b], prob[q][:, b], ACT.Exp, bias=negm[q][:, b:b + 1],
                                              accum_out=psum[q][:, b:b + 1])
                    last.then_inc(exp_done, 1)

            def step_and_tail(g, par, half):
                step(g, par, half)
                if known(g) and g == STEPS - 2:
                    inverse_root(4, slice(0, HB))

            pipeline(act, step_and_tail)

            for c in range(C):
                act.wait_ge(weff_sum, c + 1)
                act.activation(weff_hi[:, c], ffn_w[:, c], ACT.Copy).then_inc(weff_hi_done, 1)
            for half in range(2):
                bank = acc if half else misc
                for c in range(C):
                    act.wait_ge(zf_ps, C * half + c + 1)
                    act.activation(zf_hi[:, c, half * HT:(half + 1) * HT], bank[:, c], ACT.Copy).then_inc(zf_hi_done, 1)
                if half == 0:
                    inverse_root(5, slice(HB, B))

        @block.vector
        def _(dve):
            links = [0]

            def link(ins):
                links[0] += 1
                ins.then_inc(dve_chain, 1)
                dve.wait_ge(dve_chain, links[0])

            def moments(tile, bs):
                for b in bs:
                    last = dve.bn_stats(stats[:, b], tile[:, b])
                link(last)
                for b in bs:
                    last = dve.bn_aggr(mv[:, b], stats[:, b])
                link(last)

            def refine(n, part):
                dve.wait_ge(ln_exp, n)
                link(dve.tensor_tensor(tmp8[:, part], rstd[:, part], rstd[:, part], ALU.mult))
                link(dve.tensor_tensor(tmp8[:, part], tmp8[:, part], var[:, part], ALU.mult))
                link(dve.tensor_scalar(tmp8[:, part], tmp8[:, part], -0.5, 1.5, ALU.mult, ALU.add))
                link(dve.tensor_tensor(rstd[:, part], rstd[:, part], tmp8[:, part], ALU.mult))

            def norm(out, tile, b):
                return dve.tensor_scalar(out, tile, mv[:, b, 0:1], rstd[:, b:b + 1], ALU.subtract, ALU.mult)

            for c in range(C):
                dve.wait_ge(ctx_hi_done, c + 1)
                dve.tensor_tensor(wk_lo[:, c], wraw[:, c], wk_hi[:, c].bitcast(F32), ALU.subtract)
                dve.tensor_tensor(ctx_lo[:, c], ctx_raw[:, c], ctx_hi[:, c].bitcast(F32), ALU.subtract).then_inc(ctx_lo_done, 1)
            everyone = slice(0, B)
            for i in range(2):
                dve.wait_ge(x_in[i], 16)
                moments(w_tok, range(HB * i, HB * (i + 1)))
            dve.tensor_scalar(var[:], mv[:, :, 1], EPS, None, ALU.add).then_inc(ln_var, 1)
            refine(1, everyone)
            for b in range(B):
                norm(w_tok[:, b], w_tok[:, b], b).then_inc(ln1_done, 1)
            dve.wait_ge(params_in, 16 * 7)
            dve.tensor_scalar(maskadd[:], maskraw[:], 1.0, -MASKED, ALU.subtract, ALU.mult).then_inc(mask_done, 1)
            dve.tensor_reduce(anykey[:], maskraw[:], AX_X, ALU.max).then_inc(mask_done, 1)
            def softplus_max(c):
                dve.wait_ge(dt_ps, c + 1)
                dve.tensor_scalar(dt_[:, c].rearrange("p (h t) -> p h t", t=HT), misc[:, 2 * (c % 2):2 * (c % 2) + 2],
                                  dtb[:, c:c + 1], 0.0, ALU.add, ALU.max).then_inc(sp_max, 1)

            def softplus_rest(c):
                e, v = w[:, c], dA[c % 2][:, :, :].rearrange("p b s -> p (b s)")
                dve.wait_ge(sp_exp, c + 1)
                dve.wait_ge(sp_max, c + 1)
                link(dve.tensor_scalar(v, e, 1.0, -1.0, ALU.add, ALU.add))
                dve.wait_ge(sp_log, c + 1)
                link(dve.tensor_tensor(e, e, v, ALU.subtract))
                link(dve.tensor_tensor(e, e, u[:, c], ALU.add))
                dve.tensor_tensor(dt_[:, c], dt_[:, c], e, ALU.add).then_inc(sp_done, 1)
                dve.wait_ge(sp_done, c + 1)
                link(dve.tensor_tensor(u[:, c], dt_[:, c], y[:, c], ALU.mult))
                dve.tensor_scalar(y[:, c], y[:, c], dskip[:, c:c + 1], None, ALU.mult).then_inc(y_ready, 1)

            softplus_max(0)
            for c in range(C):
                if c + 1 < C:
                    softplus_max(c + 1)
                softplus_rest(c)
            for i in range(2):
                dve.memset(dA[i][:, :, 0:1], 0.0).then_inc(da_free, 1)

            def dbx(g, t, c):
                j = J * (g - 1) + C * (t + 1) + c
                dve.wait_ge(y_ready, j + 1)
                if c == 0:
                    dve.wait_ge(bc_in[(t + 1) % TRI], 16 * (g + (t + 1) // TRI))
                dve.tensor_tensor(w[:, c], u[:, c], bc[(t + 1) % TRI][:, 0], ALU.mult).then_inc(dbx_done, 1)

            def scan_step(g, t, c):
                j = J * (g - 1) + C * (t + 1) + c
                dve.wait_ge(dbx_done, j + 1)
                dve.wait_ge(da_ready, j + 1)
                dve.tensor_tensor_scan(w[:, c], dA[c % 2][:, :, :].rearrange("p b s -> p (b s)"), w[:, c], 0.0,
                                       ALU.mult, ALU.add).then_inc(da_free, 1)

            def times_c(g, t, c):
                j = J * (g - 1) + C * (t + 1) + c
                dve.wait_ge(da_free, j + 3)
                dve.tensor_tensor(w[:, c], w[:, c], bc[(t + 1) % TRI][:, 1], ALU.mult).then_inc(prod_done, 1)

            def states(g, first):
                steps = [(g, t, c) for t in range(first, TRI) for c in range(C)]
                dbx(*steps[0])
                for i, now in enumerate(steps):
                    if i + 1 < len(steps):
                        dbx(*steps[i + 1])
                    if i:
                        times_c(*steps[i - 1])
                    scan_step(*now)
                times_c(*steps[-1])

            states(0, TRI - 1)
            with dve.Fori(1, SCANS + 1) as g:
                states(g, 0)

            dve.wait_ge(x_again, 16)
            for b in range(B):
                dve.wait_ge(yt_ps, b + 1)
                dve.tensor_tensor(base[:, b], base[:, b], misc[:, b % 4], ALU.add).then_inc(x1_done, 1)
            dve.wait_ge(x1_done, B)
            moments(base, range(B))
            dve.tensor_scalar(var[:], mv[:, :, 1], EPS, None, ALU.add).then_inc(ln_var, 1)
            refine(2, everyone)
            for b in range(B):
                last = norm(w_tok[:, b], base[:, b], b)
            link(last)
            moments(w_tok, range(B))
            link(dve.tensor_tensor(tmp8[:], mv[:, :, 0], mv[:, :, 0], ALU.mult))
            link(dve.tensor_tensor(tmp8[:], tmp8[:], mv[:, :, 1], ALU.add))
            dve.tensor_scalar(var[:], tmp8[:], EPS, None, ALU.add).then_inc(ln_var, 1)
            for b in range(B):
                last = dve.tensor_tensor(base[:, b], base[:, b], w_tok[:, b], ALU.add)
            link(last)
            refine(3, everyone)
            for b in range(B):
                dve.tensor_scalar(w_tok[:, b], w_tok[:, b], rstd[:, b:b + 1], None, ALU.mult).then_inc(zn_done, 1)
            for c in range(C):
                dve.wait_ge(z_hi_done, c + 1)
                dve.scalar_tensor_tensor(z_lo[:, c].rearrange("p (h t) -> p h t", t=HT), misc[:, 2 * (c % 2):2 * (c % 2) + 2],
                                         lnw[:, c:c + 1], z_hi[:, c].bitcast(F32).rearrange("p (h t) -> p h t", t=HT),
                                         ALU.mult, ALU.subtract).then_inc(z_lo_done, 1)

            def step(g, par, half):
                p = par % 2
                if runs(g - 2):
                    sh = (g - 2) // H if known(g) else half
                    dve.wait_ge(exp_done, g - 1)
                    dve.reciprocal(rec[p][:], psum[p][:]).then_inc(rec_done, 1)
                    dve.wait_ge(rec_done, g - 1)
                    dve.tensor_tensor(rec[p][:], rec[p][:], anykey[:, sh * HB:(sh + 1) * HB], ALU.mult).then_inc(recv_done, 1)
                    dve.wait_ge(recv_done, g - 1)
                    dve.tensor_tensor(prob[p][:], prob[p][:], rec[p][:, :].unsqueeze(2).to_broadcast([P, HB, S]),
                                      ALU.mult).then_inc(p_ready, 1)
                    if known(g) and g >= STEPS:
                        sum_weff(2 * (g - STEPS))
                    dve.wait_ge(t_done, g - 1)
                    if not known(g) or g > 3:
                        dve.wait_ge(pv_done, g - 3)
                    dve.tensor_copy(pt_sb[p][:, :, :].rearrange("p b q -> p (b q)"), psT).then_inc(pt_evac, 1)
                if runs(g - 1):
                    q = 1 - p
                    dve.wait_ge(s_done, g)
                    dve.wait_ge(bm_done, g)
                    if not known(g) or g > 2:
                        dve.wait_ge(t_done, g - 2)
                    dve.tensor_tensor(prob[q][:], psS.rearrange("p (b k) -> p b k", k=S), bm[q][:], ALU.add).then_inc(sb_done, 1)
                    dve.wait_ge(sb_done, g)
                    dve.tensor_reduce(negm[q][:], prob[q][:], AX_X, ALU.max, negate=True).then_inc(mx_done, 1)
                if runs(g - 2):
                    dve.wait_ge(ot_hi_done, g - 1)
                    dve.tensor_tensor(ot_lo[p][:], psO, ot_hi[p][:].bitcast(F32), ALU.subtract).then_inc(ot_lo_done, 1)
                    if known(g) and g >= STEPS:
                        sum_weff(2 * (g - STEPS) + 1)
                if known(g) and g - 3 == H - 1:
                    add_sums(0)

            def add_sums(half):
                dve.wait_ge(o_done, (half + 1) * H)
                for b in range(HB):
                    dve.tensor_tensor(base[:, half * HB + b], base[:, half * HB + b], acc[:, b], ALU.add).then_inc(x2_done, 1)

            def sum_weff(c):
                dve.wait_ge(weff_ps, c + 1)
                dve.tensor_tensor(ffn_w[:, c], ffn_w[:, c], psQ, ALU.add).then_inc(weff_sum, 1)

            def moments_3(half):
                part = slice(half * HB, (half + 1) * HB)
                dve.wait_ge(x2_done, (half + 1) * HB)
                moments(base, range(half * HB, (half + 1) * HB))
                dve.tensor_scalar(var[:, part], mv[:, part, 1], EPS, None, ALU.add).then_inc(ln_var, 1)

            def norm_3(half):
                refine(4 + half, slice(half * HB, (half + 1) * HB))
                for b in range(half * HB, (half + 1) * HB):
                    norm(xn[:, b], base[:, b], b).then_inc(ln3_done, 1)

            def add_bias(half):
                dve.wait_ge(ln3_done, (half + 1) * HB)
                for b in range(half * HB, (half + 1) * HB):
                    last = dve.tensor_tensor(base[:, b], base[:, b], ffn_b[:], ALU.add)
                link(last)

            def f_split(half):
                bank = acc if half else misc
                for c in range(C):
                    dve.wait_ge(zf_hi_done, C * half + c + 1)
                    dve.tensor_tensor(zf_lo[:, c, half * HT:(half + 1) * HT], bank[:, c],
                                      zf_hi[:, c, half * HT:(half + 1) * HT].bitcast(F32), ALU.subtract).then_inc(zf_lo_done, 1)

            def finish(half):
                for b in range(half * HB, (half + 1) * HB):
                    dve.wait_ge(f_done, b + 1)
                    dve.tensor_tensor(base[:, b], base[:, b], misc[:, b % HB], ALU.add).then_inc(out_ready, 1)

            def step_and_tail(g, par, half):
                step(g, par, half)
                if known(g) and g == STEPS - 2:
                    dve.wait_ge(ffn_in, 16 * 6)
                    moments_3(0)
                if known(g) and g == STEPS - 1:
                    norm_3(0)
                    add_bias(0)

            pipeline(dve, step_and_tail)
            for c in range(C):
                dve.wait_ge(weff_hi_done, c + 1)
                dve.tensor_tensor(weff_lo[:, c], ffn_w[:, c], weff_hi[:, c].bitcast(F32), ALU.subtract).then_inc(weff_lo_done, 1)
            f_split(0)
            add_sums(1)
            moments_3(1)
            norm_3(1)
            finish(0)
            add_bias(1)
            f_split(1)
            finish(1)

        @block.gpsimd
        def _(pool):
            pool.memset(ident[:], 0.0).then_inc(ident_set, 1)
            pool.wait_ge(ident_set, 1)
            pool.affine_select(out=ident[:], in_=ident[:], compare_op=ALU.not_equal, fill=1.0, base=0,
                               pattern=[[-1, P]], channel_multiplier=1).then_inc(ident_done, 1)

            def low_w(m, hi, lo):
                pool.wait_ge(w_hi_done, m)
                pool.tensor_tensor(lo[:], wraw[:], hi[:].bitcast(F32), ALU.subtract).then_inc(w_lo_done, 1)

            def add_y(g, t, c):
                j = J * (g - 1) + C * (t + 1) + c
                pool.wait_ge(prod_done, j + 1)
                pool.tensor_tensor(y[:, c], y[:, c], w[:, c], ALU.add).then_inc(y_ready, 1)

            low_w(1, wv_hi, wv_lo)
            low_w(2, wk_hi, wk_lo)
            for c in range(C):
                add_y(0, TRI - 1, c)
            with pool.Fori(1, SCANS + 1) as g:
                low_w(2 * g + 1, wv_hi, wv_lo)
                for i in range(J):
                    if i == J // 2:
                        low_w(2 * g + 2, wk_hi, wk_lo)
                    add_y(g, i // C, i % C)
            for g in range(SCANS + 1, NG):
                low_w(2 * g + 1, wv_hi, wv_lo)
                if g + 1 < NG:
                    low_w(2 * g + 2, wk_hi, wk_lo)

            def low_wq(g, p):
                pool.wait_ge(wq_hi_done, g + 1)
                pool.tensor_tensor(wq_lo[p][:], wq_raw[p][:], wq_hi[p][:].bitcast(F32), ALU.subtract).then_inc(wq_lo_done, 1)

            low_wq(0, 0)

            def step(g, par, half):
                p = par % 2
                if runs(g) and runs(g + 1):
                    low_wq(g + 1, 1 - p)
                if runs(g):
                    sh = g // H if known(g) else half
                    if known(g) and g == 0:
                        pool.wait_ge(mask_done, 1)
                    pool.wait_ge(kb_in[p], in_count(g, p, 32))
                    if not known(g) or g >= 2:
                        pool.wait_ge(sb_done, g - 1)
                    pool.tensor_tensor(bm[p][:], bias[p][:, :].unsqueeze(1).to_broadcast([P, HB, S]),
                                       maskadd[:, sh * HB:(sh + 1) * HB], ALU.add).then_inc(bm_done, 1)
                if runs(g - 2):
                    pool.wait_ge(wo_hi_done, g - 1)
                    pool.tensor_tensor(wo_lo[p][:], wo_raw[p][:], wo_hi[p][:].bitcast(F32), ALU.subtract).then_inc(wo_lo_done, 1)

            def step_and_tail(g, par, half):
                step(g, par, half)
                if known(g) and g == H:
                    pool.wait_ge(ffn_in, 16 * 6)
                    for e in range(ER):
                        pool.tensor_scalar(eb_sb[:, e], eb_sb[:, e], eprob[:, e:e + 1], 1.0, ALU.mult, ALU.mult).then_inc(eb_done, 1)

            pipeline(pool, step_and_tail)


def kernel(**inputs):
    import numpy as np
    import concourse.bacc as bacc
    from concourse.bass_utils import run_bass_kernel_spmd as run

    x = np.asarray(inputs["x"])

    def chunks(m):
        m = np.asarray(m)
        return m.reshape(m.shape[0] // P, P, -1).transpose(1, 0, 2)

    def groups(m, heads):
        m = np.asarray(m)
        return m.reshape(H // heads, heads * P, C, P).transpose(0, 3, 2, 1)

    arrays = {
        "x": x,
        "ctxT": chunks(np.asarray(inputs["ctx_4096"]).reshape(T, D).T),
        "mask": inputs["mask_BxSxS2_bk0"],
        "A_log": chunks(inputs["L0_attn_A_log"]),
        "D": np.asarray(inputs["L0_attn_D"]).reshape(C, P).T,
        "dt_b": np.asarray(inputs["L0_attn_dt_proj_b"]).reshape(C, P).T,
        "xp_w": chunks(np.asarray(inputs["L0_attn_x_proj_w"]).T),
        "dt_w": np.asarray(inputs["L0_attn_dt_proj_w"]).T,
        "ln_w": np.asarray(inputs["L0_xattn_ln_weight"]).reshape(C, P).T,
        "pbias": inputs["L0_xattn_position_bias"],
        "wq": groups(inputs["L0_xattn_w_q"], 1),
        "wk": groups(inputs["L0_xattn_w_k"], G),
        "wv": groups(inputs["L0_xattn_w_v"], G),
        "wo": np.asarray(inputs["L0_xattn_w_out"]).T.reshape(H, P, D),
        "ffn_w": chunks(np.asarray(inputs["L0_ffn_W"]).T),
        "ffn_a": chunks(np.asarray(inputs["L0_ffn_A"]).reshape(-1, D)),
        "ffn_bw": chunks(np.asarray(inputs["L0_ffn_B"]).transpose(0, 2, 1).reshape(-1, D)),
        "ffn_b": inputs["L0_ffn_b"],
        "probs": np.repeat(np.asarray(inputs["L0_ffn_probs"]), P * ER // E).reshape(-1, 1),
    }
    nc = bacc.Bacc("TRN2", target_bir_lowering=False, num_devices=1)
    a, given = {}, {}
    for name, v in arrays.items():
        v = np.ascontiguousarray(v)
        given[f"in_{name}"] = v
        a[name] = nc.dram_tensor(f"in_{name}", v.shape, mybir.dt.from_np(v.dtype), kind="ExternalInput").ap()
    a["out"] = nc.dram_tensor("out_x", x.shape, F32, kind="ExternalOutput").ap()
    decoder_layer(nc, a)
    r = run(nc, [given], core_ids=[0])
    return r.results[0]["out_x"]
```

```python
from contextlib import ExitStack

import concourse.bass as bass
from concourse import mybir

F32 = mybir.dt.float32
F32R = mybir.dt.float32r
BF16 = mybir.dt.bfloat16
U8 = mybir.dt.uint8
ALU = mybir.AluOpType
ACT = mybir.ActivationFunctionType
AX_X = mybir.AxisListType.X

P = 128
B = 8
S = 128
D = 512
C = D // P
T = B * S
H = 32
N = 16
R = 16
RX = R + 2 * N
G = 4
NG = H // G
HB = B // 2
HT = HB * S
KP = 2 * G
STEPS = 2 * H
TRI = 3
SCANS = N // TRI
REST = N - TRI * SCANS
J = TRI * C
E = 16
ER = E * 16 // P
WARM = 24
V_LN2 = 4
K_LN2 = 2
KZ = 5
EPS = 1e-5
MASKED = -1e30


def decoder_layer(nc, a):
    k_dram = nc.dram_tensor("k_scratch", (STEPS, P, HT), F32, kind="Internal").ap()
    v_dram = nc.dram_tensor("v_scratch", (STEPS, P, HT), F32, kind="Internal").ap()
    xp_dram = nc.dram_tensor("xp_scratch", (2, N, T), F32, kind="Internal").ap()
    v_dram_g = v_dram.rearrange("(q h) p x -> q p h x", h=G)

    with ExitStack() as whole:
        def sb(stack, name, shape, dt=F32, side="left"):
            return stack.enter_context(nc.sbuf_tensor(name, shape, dt, side=side))

        acc = whole.enter_context(nc.psum_tensor("acc", [P, 4, 512], F32))
        misc = whole.enter_context(nc.psum_tensor("misc", [P, 4, 512], F32))
        psQ, psS, psT, psO = (misc[:, i, :] for i in range(4))

        base = sb(whole, "base", [P, B, D])
        ident = sb(whole, "ident", [P, P])
        maskadd = sb(whole, "maskadd", [P, B, S], BF16)
        anykey = sb(whole, "anykey", [P, B])
        lnw = sb(whole, "lnw", [P, C])
        stats = sb(whole, "stats", [P, B, 6])
        mv = sb(whole, "mv", [P, B, 2])
        var = sb(whole, "var", [P, B])
        rstd = sb(whole, "rstd", [P, B])
        tmp8 = sb(whole, "tmp8", [P, B])

        with ExitStack() as low:
            ctx_hi = sb(low, "ctx_hi", [P, C, T], F32R, "right")
            ctx_lo = sb(low, "ctx_lo", [P, C, T], F32R, "right")
            wraw = sb(low, "wraw", [P, C, G * P], F32, "right")
            wk_hi = sb(low, "wk_hi", [P, C, G * P], F32R, "right")
            wk_lo = sb(low, "wk_lo", [P, C, G * P], F32R, "right")
            wv_hi = sb(low, "wv_hi", [P, C, G * P], F32R, "right")
            wv_lo = sb(low, "wv_lo", [P, C, G * P], F32R, "right")
            kst = [sb(low, f"kst{i}", [P, HT], F32, "right") for i in range(2)]
            vst = [sb(low, f"vst{i}", [P, G, 2, P], F32, "right") for i in range(2)]

        with ExitStack() as tail:
            zf_hi = sb(tail, "zf_hi", [P, C, T], F32R, "right")
            zf_lo = sb(tail, "zf_lo", [P, C, T], F32R, "right")
            ffn_w = sb(tail, "ffn_w", [P, C, D], F32, "right")
            weff_hi = sb(tail, "weff_hi", [P, C, D], F32R, "right")
            weff_lo = sb(tail, "weff_lo", [P, C, D], F32R, "right")
            ea_sb = sb(tail, "ea_sb", [P, ER, D], F32, "right")
            eb_sb = sb(tail, "eb_sb", [P, ER, D], F32, "right")
            eprob = sb(tail, "eprob", [P, ER], F32, "right")
            ffn_b = sb(tail, "ffn_b", [P, D], F32, "right")
            xn = sb(tail, "xn", [P, B, D], F32, "right")

        with ExitStack() as scan:
            dt_ = sb(scan, "dt_", [P, C, T])
            u = sb(scan, "u", [P, C, T])
            bc = [sb(scan, f"bc{i}", [P, 2, T]) for i in range(TRI)]
            dA = [sb(scan, f"dA{i}", [P, B, S]) for i in range(2)]
            y = sb(scan, "y", [P, C, T])
            w = sb(scan, "w", [P, C, T])
            negA = sb(scan, "negA", [P, C, N])
            dskip = sb(scan, "dskip", [P, C])
            dtb = sb(scan, "dtb", [P, C])
            xpw = sb(scan, "xpw", [P, C, RX])
            dtw = sb(scan, "dtw", [R, D])
            maskraw = sb(scan, "maskraw", [P, B, S], U8)

        pair = range(2)
        z_hi = sb(whole, "z_hi", [P, C, T], F32R)
        z_lo = sb(whole, "z_lo", [P, C, T], F32R)
        wq_raw = [sb(whole, f"wq_raw{i}", [P, C, P]) for i in pair]
        wq_hi = [sb(whole, f"wq_hi{i}", [P, C, P], F32R) for i in pair]
        wq_lo = [sb(whole, f"wq_lo{i}", [P, C, P], F32R) for i in pair]
        wo_raw = [sb(whole, f"wo_raw{i}", [P, D]) for i in pair]
        wo_hi = [sb(whole, f"wo_hi{i}", [P, D], F32R) for i in pair]
        wo_lo = [sb(whole, f"wo_lo{i}", [P, D], F32R) for i in pair]
        k_sb = [sb(whole, f"k_sb{i}", [P, HT]) for i in pair]
        v_sb = [sb(whole, f"v_sb{i}", [P, HB, P]) for i in pair]
        q_sb = [sb(whole, f"q_sb{i}", [P, HT]) for i in pair]
        prob = [sb(whole, f"prob{i}", [P, HB, S]) for i in pair]
        pt_sb = [sb(whole, f"pt_sb{i}", [P, HB, S]) for i in pair]
        bias = [sb(whole, f"bias{i}", [P, S]) for i in pair]
        bm = [sb(whole, f"bm{i}", [P, HB, S]) for i in pair]
        negm = [sb(whole, f"negm{i}", [P, HB]) for i in pair]
        psum = [sb(whole, f"psum{i}", [P, HB]) for i in pair]
        rec = [sb(whole, f"rec{i}", [P, HB]) for i in pair]
        ot_hi = [sb(whole, f"ot_hi{i}", [P, HT], F32R) for i in pair]
        ot_lo = [sb(whole, f"ot_lo{i}", [P, HT], F32R) for i in pair]

        w_tok = w[:, :, :].rearrange("p c (h d) -> p (c h) d", d=D)
        xp_sb = base[:, 0:2, :].rearrange("p h t -> p (h t)")
        ctx_raw = base[:, :, :].rearrange("p (c h) t -> p c (h t)", c=C)

        def sem(name):
            return whole.enter_context(nc.semaphore(name))

        x_in = [sem(f"x_in{i}") for i in range(2)]
        ctx_in = [sem(f"ctx_in{i}") for i in range(C)]
        params_in, x_again, wraw_in = sem("params_in"), sem("x_again"), sem("wraw_in")
        k_stored = [sem(f"k_stored{i}") for i in range(2)]
        v_stored = [sem(f"v_stored{i}") for i in range(2)]
        xp_stored = sem("xp_stored")
        bc_in = [sem(f"bc_in{i}") for i in range(TRI)]
        wq_in = [sem(f"wq_in{i}") for i in pair]
        wo_in = [sem(f"wo_in{i}") for i in pair]
        kb_in = [sem(f"kb_in{i}") for i in pair]
        v_in = [sem(f"v_in{i}") for i in pair]
        ffn_in, out_stored = sem("ffn_in"), sem("out_stored")
        ident_set, ident_done, mask_done = sem("ident_set"), sem("ident_done"), sem("mask_done")
        ctx_hi_done, ctx_lo_done = sem("ctx_hi_done"), sem("ctx_lo_done")
        wk_hi_0, wk_lo_0 = sem("wk_hi_0"), sem("wk_lo_0")
        w_hi_done, w_lo_done = sem("w_hi_done"), sem("w_lo_done")
        k_done, k_evac, v_done, v_evac = sem("k_done"), sem("k_evac"), sem("v_done"), sem("v_evac")
        ln_var, ln_log, ln_exp = sem("ln_var"), sem("ln_log"), sem("ln_exp")
        ln1_done = sem("ln1_done")
        xt_ps, xt_evac, xp_ps, xp_evac, dt_ps = sem("xt_ps"), sem("xt_evac"), sem("xp_ps"), sem("xp_evac"), sem("dt_ps")
        sp_max, sp_abs, sp_exp = sem("sp_max"), sem("sp_abs"), sem("sp_exp")
        sp_log, sp_rest, sp_done, u_done = sem("sp_log"), sem("sp_rest"), sem("sp_done"), sem("u_done")
        a_exp, a_neg = sem("a_exp"), sem("a_neg")
        y_ready, da_free, da_ready = sem("y_ready"), sem("da_free"), sem("da_ready")
        dbx_done, prod_done = sem("dbx_done"), sem("prod_done")
        yt_ps, x1_done, zn_done, zt_ps = sem("yt_ps"), sem("x1_done"), sem("zn_done"), sem("zt_ps")
        z_hi_done, z_lo_done = sem("z_hi_done"), sem("z_lo_done")
        wq_hi_done, wq_lo_done = sem("wq_hi_done"), sem("wq_lo_done")
        wo_hi_done, wo_lo_done = sem("wo_hi_done"), sem("wo_lo_done")
        q_done, q_evac, s_done, sb_done = sem("q_done"), sem("q_evac"), sem("s_done"), sem("sb_done")
        bm_done = sem("bm_done")
        mx_done, exp_done, rec_done, recv_done = sem("mx_done"), sem("exp_done"), sem("rec_done"), sem("recv_done")
        p_ready, t_done, pt_evac, pv_done = sem("p_ready"), sem("t_done"), sem("pt_evac"), sem("pv_done")
        ot_hi_done, ot_lo_done, o_done, x2_done = sem("ot_hi_done"), sem("ot_lo_done"), sem("o_done"), sem("x2_done")
        eb_done, weff_ps, weff_sum = sem("eb_done"), sem("weff_ps"), sem("weff_sum")
        weff_hi_done, weff_lo_done = sem("weff_hi_done"), sem("weff_lo_done")
        ln3_done, bias_added, zf_ps = sem("ln3_done"), sem("bias_added"), sem("zf_ps")
        zf_hi_done, zf_lo_done, f_done, out_ready = sem("zf_hi_done"), sem("zf_lo_done"), sem("f_done"), sem("out_ready")
        dve_chain = sem("dve_chain")

        block = whole.enter_context(nc.Block())

        def pipeline(eng, step, behind=lambda g: None):
            for g in range(4):
                step(g, g, 0)
                behind(g)
            with eng.Fori(2, H // 2 - 1) as i:
                for p in pair:
                    step(2 * i + p, p, 0)
            for g in range(H - 2, H + 4):
                step(g, g, g // H)
            with eng.Fori(H // 2 + 2, H - 1) as i:
                for p in pair:
                    step(2 * i + p, p, 1)
            for g in range(STEPS - 2, STEPS + 3):
                step(g, g, 1)

        def known(g):
            return isinstance(g, int)

        def runs(g):
            return not known(g) or 0 <= g < STEPS

        def in_count(g, p, n):
            return n * (g // 2 + 1) if known(g) else n // 2 * (g - p) + n

        @block.sync
        def _(sp):
            for c in range(C):
                sp.dma_start(wraw[:, c], a["wk"][0][:, c]).then_inc(ctx_in[c], 16)
                sp.dma_start(ctx_raw[:, c], a["ctxT"][:, c]).then_inc(ctx_in[c], 16)
            for i in range(2):
                sp.dma_start(w_tok[:, HB * i:HB * (i + 1)],
                             a["x"][HB * i:HB * (i + 1)].rearrange("b t d -> t b d")).then_inc(x_in[i], 16)
            for dst, src in ((negA, "A_log"), (dskip, "D"), (dtb, "dt_b"), (xpw, "xp_w"), (dtw, "dt_w"), (lnw, "ln_w")):
                sp.dma_start(dst[:], a[src]).then_inc(params_in, 16)
            sp.dma_start(maskraw[:], a["mask"].rearrange("b q k -> q b k")).then_inc(params_in, 16)

            def k_store(g, j):
                sp.wait_ge(k_evac, KP * g + j + 1)
                sp.dma_start(k_dram[H * (j % 2) + G * g + j // 2], kst[j % 2][:]).then_inc(k_stored[j % 2], 16)

            def v_store(g, q):
                sp.wait_ge(v_evac, B * g + 2 * q + 2)
                sp.dma_start(v_dram_g[NG * (q // 2) + g, :, :, 2 * P * (q % 2):2 * P * (q % 2 + 1)],
                             vst[q % 2][:, :, :, :].rearrange("p h b d -> p h (b d)")).then_inc(v_stored[q % 2], 16)

            def load_w(w_of_group, c):
                sp.dma_start(wraw[:, c], w_of_group[:, c]).then_inc(wraw_in, 16)

            def k_group(g, more, start=3):
                for j in range(KP):
                    k_store(g, j)
                    if more and start <= j < start + C:
                        if j == start:
                            sp.wait_ge(w_lo_done, 2 * g + 1)
                        load_w(a["wk"][g + 1], j - start)

            def v_group(g, more):
                for q in range(4):
                    v_store(g, q)
                    if more and 1 <= q < 3:
                        if q == 1:
                            sp.wait_ge(w_lo_done, 2 * g + 2)
                        for c in range(2 * (q - 1), 2 * q):
                            load_w(a["wv"][g + 1], c)

            for c in range(C):
                sp.wait_ge(wk_lo_0, c + 1)
                load_w(a["wv"][0], c)
            k_group(0, True, KP - C)
            v_group(0, True)
            sp.wait_ge(dt_ps, C)
            sp.wait_ge(xp_stored, 16)
            sp.dma_start(base[:], a["x"].rearrange("b t d -> t b d")).then_inc(x_again, 16)
            with sp.Fori(1, SCANS + 1) as g:
                k_group(g, True)
                v_group(g, True)

            def load_wq(h, p):
                sp.dma_start(wq_raw[p][:], a["wq"][h]).then_inc(wq_in[p], 16)

            def load_kb(g, h, p):
                sp.dma_start(k_sb[p][:], k_dram[g]).then_inc(kb_in[p], 16)
                sp.dma_start(bias[p][:], a["pbias"][h]).then_inc(kb_in[p], 16)

            k_group(NG - 2, True)
            sp.wait_ge(prod_done, C * N)
            for g in range(2):
                load_wq(g, g)
            v_group(NG - 2, True)
            k_group(NG - 1, False)
            v_store(NG - 1, 0)
            for i in range(2):
                sp.wait_ge(k_stored[i], 16 * KP // 2 * NG)
            sp.wait_ge(v_stored[1], 16 * 2 * (NG - 1))
            sp.wait_ge(v_stored[0], 16 * 2 * (NG - 1) + 16)
            sp.wait_ge(yt_ps, B)
            load_kb(0, 0, 0)

            def head(g, half):
                return g % H if known(g) else g - H * half

            def step(g, par, half):
                p = par % 2
                if runs(g) and runs(g + 2):
                    sp.wait_ge(wq_lo_done, g + 1)
                    load_wq(head(g + 2, half), p)
                if runs(g) and runs(g + 1):
                    if not known(g) or g >= 1:
                        sp.wait_ge(sb_done, g)
                    load_kb(g + 1, head(g + 1, half), 1 - p)
                if runs(g):
                    if not known(g) or g >= 2:
                        sp.wait_ge(pv_done, g - 1)
                    sp.dma_start(v_sb[p][:, :, :].rearrange("p b d -> p (b d)"), v_dram[g]).then_inc(v_in[p], 16)
                    if not known(g) or g >= 2:
                        sp.wait_ge(wo_lo_done, g - 1)
                    sp.dma_start(wo_raw[p][:], a["wo"][head(g, half)]).then_inc(wo_in[p], 16)

            def behind(g):
                if g == 0:
                    v_store(NG - 1, 1)
                if g == 1:
                    v_store(NG - 1, 2)
                if g == 2:
                    v_store(NG - 1, 3)
                    for i in range(2):
                        sp.wait_ge(v_stored[i], 16 * 2 * NG)
                    sp.wait_ge(v_done, B * NG)
                    sp.dma_start(ffn_w[:], a["ffn_w"]).then_inc(ffn_in, 16)
                if g == 3:
                    sp.dma_start(ea_sb[:], a["ffn_a"]).then_inc(ffn_in, 16)
                    sp.dma_start(eb_sb[:], a["ffn_bw"]).then_inc(ffn_in, 16)
                    sp.dma_start(ffn_b[:], a["ffn_b"].partition_broadcast(P)).then_inc(ffn_in, 16)
                    for e in range(ER):
                        sp.dma_start(eprob[:, e:e + 1], a["probs"][P * e:P * (e + 1), :]).then_inc(ffn_in, 16)

            pipeline(sp, step, behind)
            for b in range(B):
                sp.wait_ge(out_ready, b + 1)
                sp.dma_start(a["out"][b], base[:, b]).then_inc(out_stored, 16)
            sp.wait_ge(out_stored, 16 * B)

        @block.tensor
        def _(pe):
            def three(out, w_hi, w_lo, m_hi, m_lo, first, last):
                pe.matmul(out, w_hi, m_hi, start=first, stop=False)
                pe.matmul(out, w_hi, m_lo, start=False, stop=False)
                return pe.matmul(out, w_lo, m_hi, start=False, stop=last)

            def k_part(j, bank, c):
                hd, half = slice(j // 2 * P, (j // 2 + 1) * P), slice(j % 2 * HT, (j % 2 + 1) * HT)
                return three(acc[:, bank], wk_hi[:, c, hd], wk_lo[:, c, hd], ctx_hi[:, c, half], ctx_lo[:, c, half],
                             c == 0, c == C - 1)

            def k_sum(g, j):
                pe.wait_ge(k_evac, KP * g + j - 1)
                for c in range(C):
                    mm = k_part(j, j % 2, c)
                mm.then_inc(k_done, 1)

            def v_sum(g, b, first=False):
                if not first or b >= 2:
                    pe.wait_ge(v_evac, B * g + b - 1)
                tok = slice(b * S, (b + 1) * S)
                for c in range(C):
                    mm = three(acc[:, 2 + b % 2], ctx_hi[:, c, tok], ctx_lo[:, c, tok], wv_hi[:, c], wv_lo[:, c],
                               c == 0, c == C - 1)
                mm.then_inc(v_done, 1)

            pe.wait_ge(ident_done, 1)
            for i in range(WARM):
                pe.transpose(misc[:, i % 4, 0:P], ident[:], ident[:])
            for c in range(C):
                pe.wait_ge(ctx_hi_done, c + 1)
                for j in range(4):
                    w_part, m_part = slice(j // 2 * P, (j // 2 + 1) * P), slice(j % 2 * HT, (j % 2 + 1) * HT)
                    pe.matmul(acc[:, j], wk_hi[:, c, w_part], ctx_hi[:, c, m_part], start=(c == 0), stop=False)
                pe.wait_ge(ctx_lo_done, c + 1)
                pe.wait_ge(wk_lo_0, c + 1)
                for j in range(4):
                    w_part, m_part = slice(j // 2 * P, (j // 2 + 1) * P), slice(j % 2 * HT, (j % 2 + 1) * HT)
                    pe.matmul(acc[:, j], wk_hi[:, c, w_part], ctx_lo[:, c, m_part], start=False, stop=False)
                    mm = pe.matmul(acc[:, j], wk_lo[:, c, w_part], ctx_hi[:, c, m_part], start=False, stop=(c == C - 1))
                    if c == C - 1:
                        mm.then_inc(k_done, 1)

            def k_sum_0(j):
                pe.wait_ge(k_evac, j - 3 if j < 6 else j - 1)
                for c in range(C):
                    mm = k_part(j, j % 2, c)
                mm.then_inc(k_done, 1)

            def dt_proj(c):
                if c >= 2:
                    pe.wait_ge(sp_abs, c - 1)
                for half in range(2):
                    mm = pe.matmul(misc[:, 2 * (c % 2) + half], dtw[:, c * P:(c + 1) * P],
                                   xp_sb[0:R, half * HT:(half + 1) * HT], start=True, stop=True)
                mm.then_inc(dt_ps, 1)

            def x_chunk(c):
                if c >= 2:
                    pe.wait_ge(xt_evac, c)
                for b in range(B):
                    if c == 0:
                        pe.wait_ge(ln1_done, b + 1)
                    mm = pe.transpose(misc[:, 2 * min(c, 1) + b // HB, b % HB * S:(b % HB + 1) * S],
                                      w_tok[:, b, c * P:(c + 1) * P], ident[:])
                mm.then_inc(xt_ps, 1)

            def x_proj(c):
                pe.wait_ge(xt_evac, c + 1)
                for half in range(2):
                    mm = pe.matmul(misc[0:RX, half], xpw[:, c], y[:, c, half * HT:(half + 1) * HT],
                                   start=(c == 0), stop=(c == C - 1))
                if c == C - 1:
                    mm.then_inc(xp_ps, 1)

            k_sum_0(4)
            k_sum_0(5)
            x_chunk(0)
            x_chunk(1)
            k_sum_0(6)
            x_chunk(2)
            pe.wait_ge(params_in, 16 * 7)
            x_proj(0)
            x_proj(1)
            x_chunk(3)
            x_proj(2)
            x_proj(3)
            k_sum_0(7)
            pe.wait_ge(w_lo_done, 1)
            v_sum(0, 0, True)
            pe.wait_ge(xp_evac, 1)
            for c in range(2):
                dt_proj(c)
            v_sum(0, 1, True)
            for c in range(2, C):
                dt_proj(c)
            for b in range(2, B):
                v_sum(0, b, True)

            def k_group(g, js):
                pe.wait_ge(w_lo_done, 2 * g)
                for j in js:
                    k_sum(g, j)

            def v_group(g, bs=range(B)):
                pe.wait_ge(w_lo_done, 2 * g + 1)
                for b in bs:
                    v_sum(g, b)

            with pe.Fori(1, SCANS + 1) as g:
                k_group(g, range(KP))
                v_group(g)

            k_group(NG - 2, range(KP))
            pe.wait_ge(y_ready, C * N + C)
            for b in range(B):
                if b >= 4:
                    pe.wait_ge(x1_done, b - 3)
                for c in range(C):
                    mm = pe.transpose(misc[:, b % 4, c * P:(c + 1) * P], y[:, c, b * S:(b + 1) * S], ident[:])
                mm.then_inc(yt_ps, 1)
            v_group(NG - 2)
            k_group(NG - 1, range(KZ))
            for c in range(C):
                if c >= 2:
                    pe.wait_ge(z_lo_done, c - 1)
                for b in range(B):
                    if c == 0:
                        pe.wait_ge(zn_done, b + 1)
                    mm = pe.transpose(misc[:, 2 * (c % 2) + b // HB, b % HB * S:(b % HB + 1) * S],
                                      w_tok[:, b, c * P:(c + 1) * P], ident[:])
                mm.then_inc(zt_ps, 1)
                if KZ + c < KP:
                    k_sum(NG - 1, KZ + c)
                else:
                    v_group(NG - 1, [KZ + c - KP])
            v_group(NG - 1, range(KZ + C - KP, 2))
            pe.wait_ge(z_lo_done, C)

            def weff_sum_of(c):
                if c == 0:
                    pe.wait_ge(eb_done, ER)
                    pe.wait_ge(q_evac, STEPS)
                else:
                    pe.wait_ge(weff_sum, c)
                for e in range(ER):
                    mm = pe.matmul(psQ, ea_sb[:, e, c * P:(c + 1) * P], eb_sb[:, e], start=(e == 0), stop=(e == ER - 1))
                mm.then_inc(weff_ps, 1)

            def f_input(half, *free):
                bank = acc if half else misc
                for c in range(C):
                    pe.wait_ge(*free[c])
                    for b in range(HB):
                        if c == 0:
                            pe.wait_ge(ln3_done, half * HB + b + 1)
                        mm = pe.transpose(bank[:, c, b * S:(b + 1) * S], xn[:, half * HB + b, c * P:(c + 1) * P], ident[:])
                    mm.then_inc(zf_ps, 1)

            def step(g, par, half):
                p = par % 2
                if known(g) and STEPS <= g <= STEPS + 1:
                    weff_sum_of(2 * (g - STEPS))
                if known(g) and g == STEPS + 2:
                    f_input(0, (weff_sum, C), (sb_done, STEPS), (pt_evac, STEPS), (ot_lo_done, STEPS))
                if runs(g):
                    tok = slice(half * HT, (half + 1) * HT)
                    pe.wait_ge(wq_lo_done, g + 1)
                    if not known(g) or g:
                        pe.wait_ge(q_evac, g)
                    for c in range(C):
                        mm = three(psQ, wq_hi[p][:, c], wq_lo[p][:, c], z_hi[:, c, tok], z_lo[:, c, tok],
                                   c == 0, c == C - 1)
                    mm.then_inc(q_done, 1)
                if runs(g - 2):
                    pe.wait_ge(p_ready, g - 1)
                    if not known(g) or g > 2:
                        pe.wait_ge(pt_evac, g - 2)
                    for b in range(HB):
                        mm = pe.transpose(psT[:, b * S:(b + 1) * S], prob[p][:, b], ident[:])
                    mm.then_inc(t_done, 1)
                if runs(g - 1):
                    pe.wait_ge(q_evac, g)
                    pe.wait_ge(kb_in[1 - p], in_count(g - 1, 1 - p, 32))
                    if not known(g) or g > 1:
                        pe.wait_ge(sb_done, g - 1)
                    for b in range(HB):
                        mm = pe.matmul(psS[:, b * S:(b + 1) * S], q_sb[1 - p][:, b * S:(b + 1) * S],
                                       k_sb[1 - p][:, b * S:(b + 1) * S], start=True, stop=True)
                    mm.then_inc(s_done, 1)
                if known(g) and STEPS <= g <= STEPS + 1:
                    weff_sum_of(2 * (g - STEPS) + 1)
                if runs(g - 3):
                    h = (g - 3) % H if known(g) else 1
                    q = 1 - p
                    if known(g) and g == 3:
                        pe.wait_ge(k_evac, KP * NG)
                        pe.wait_ge(v_evac, B * NG)
                    pe.wait_ge(ot_lo_done, g - 2)
                    pe.wait_ge(wo_lo_done, g - 2)
                    for b in range(HB):
                        tok = slice(b * S, (b + 1) * S)
                        if known(g) and g - 3 == H:
                            pe.wait_ge(x2_done, b + 1)
                        mm = three(acc[:, b], ot_hi[q][:, tok], ot_lo[q][:, tok], wo_hi[q][:], wo_lo[q][:],
                                   h == 0, h == H - 1)
                    mm.then_inc(o_done, 1)
                if runs(g - 2):
                    pe.wait_ge(pt_evac, g - 1)
                    pe.wait_ge(v_in[p], in_count(g - 2, p, 16))
                    if not known(g) or g > 2:
                        pe.wait_ge(ot_lo_done, g - 2)
                    for b in range(HB):
                        mm = pe.matmul(psO[:, b * S:(b + 1) * S], v_sb[p][:, b], pt_sb[p][:, b], start=True, stop=True)
                    mm.then_inc(pv_done, 1)

            def behind(g):
                if g <= 2:
                    v_group(NG - 1, range(2 * g + 2, 2 * g + 4))

            pipeline(pe, step, behind)

            for half in range(2):
                if half:
                    f_input(1, *((x2_done, HB + c + 1) for c in range(C)))
                for b in range(half * HB, (half + 1) * HB):
                    if half:
                        pe.wait_ge(out_ready, b - HB + 1)
                    tok = slice(b * S, (b + 1) * S)
                    for c in range(C):
                        if b == half * HB:
                            if not half:
                                pe.wait_ge(weff_lo_done, c + 1)
                            pe.wait_ge(zf_lo_done, C * half + c + 1)
                        mm = three(misc[:, b % HB], zf_hi[:, c, tok], zf_lo[:, c, tok], weff_hi[:, c], weff_lo[:, c],
                                   c == 0, c == C - 1)
                    mm.then_inc(f_done, 1)

        @block.scalar
        def _(act):
            def inverse_root(n, part):
                act.wait_ge(ln_var, n)
                act.activation(tmp8[:, part], var[:, part], ACT.Ln).then_inc(ln_log, 1)
                act.wait_ge(ln_log, n)
                act.activation(rstd[:, part], tmp8[:, part], ACT.Exp, scale=-0.5).then_inc(ln_exp, 1)

            def split_w(m, hi):
                act.wait_ge(wraw_in, 16 * C * m)
                act.activation(hi[:], wraw[:], ACT.Copy).then_inc(w_hi_done, 1)

            def k_copy(g, j, first=False):
                act.wait_ge(k_done, KP * g + j + 1)
                if not first or j >= 2:
                    act.wait_ge(k_stored[j % 2], 16 * (KP // 2 * g + j // 2))
                bank = j if first and j < 4 else j % 2
                act.activation(kst[j % 2][:], acc[:, bank], ACT.Copy).then_inc(k_evac, 1)

            def v_copy(g, b, first=False):
                act.wait_ge(v_done, B * g + b + 1)
                q = b // 2
                if not first or q >= 2:
                    act.wait_ge(v_stored[q % 2], 16 * (2 * g + q // 2))
                act.activation(vst[q % 2][:, :, b % 2], acc[:, 2 + b % 2].rearrange("p (h d) -> p h d", d=P),
                               ACT.Copy).then_inc(v_evac, 1)

            def dA_exp(g, t, c):
                act.wait_ge(da_free, J * (g - 1) + C * t + c + 1)
                act.activation(dA[c % 2][:, :, 1:S], dt_[:, c].rearrange("p (b s) -> p b s", s=S)[:, :, 1:S],
                               ACT.Exp, scale=negA[:, c, bass.ds(TRI * (g - 1) + t, 1)]).then_inc(da_ready, 1)

            def load_bc(n, i):
                act.dma_start(bc[i][:], xp_dram[:, n].partition_broadcast(P)).then_inc(bc_in[i], 16)

            def group(g, states, bc_loads):
                steps = [(t, c) for t in range(states) for c in range(C)]
                copies = [(k_copy, j) for j in range(KP)] + [(v_copy, b) for b in range(B)]
                for i, (copy, j) in enumerate(copies):
                    if i == 1:
                        act.wait_ge(v_done, B * g)
                        split_w(2 * g + 1, wv_hi)
                    if i == KP:
                        act.wait_ge(k_done, KP * g + KP)
                        split_w(2 * g + 2, wk_hi)
                    if known(g) and g == SCANS + 1 and i == KP + V_LN2:
                        inverse_root(2, slice(0, B))
                    if i % 4 != 3 and steps:
                        t, c = steps.pop(0)
                        dA_exp(g, t, c)
                        if c == C - 1 and t < bc_loads:
                            load_bc(TRI * (g - 1) + t + 2, (t + 2) % TRI)
                    copy(g, j)

            for c in range(C):
                act.wait_ge(ctx_in[c], 32)
                act.activation(wk_hi[:, c], wraw[:, c], ACT.Copy).then_inc(wk_hi_0, 1)
                act.activation(ctx_hi[:, c], ctx_raw[:, c], ACT.Copy).then_inc(ctx_hi_done, 1)
            act.wait_ge(ident_done, 1)
            act.activation(anykey[:, 0:1], ident[:, 0:1], ACT.Ln, bias=1.0)
            for j in range(2):
                k_copy(0, j, True)
            inverse_root(1, slice(0, B))
            for j in range(2, 5):
                k_copy(0, j, True)
            split_w(1, wv_hi)
            k_copy(0, 5, True)

            def x_copy(c):
                act.wait_ge(xt_ps, c + 1)
                act.activation(y[:, c].rearrange("p (h t) -> p h t", t=HT), misc[:, 2 * min(c, 1):2 * min(c, 1) + 2],
                               ACT.Copy).then_inc(xt_evac, 1)

            x_copy(0)
            x_copy(1)
            k_copy(0, 6, True)
            x_copy(2)
            x_copy(3)
            act.wait_ge(params_in, 16 * 7)
            act.activation(negA[:], negA[:], ACT.Exp).then_inc(a_exp, 1)
            act.wait_ge(a_exp, 1)
            act.activation(negA[:], negA[:], ACT.Copy, scale=-1.0).then_inc(a_neg, 1)
            act.wait_ge(xp_ps, 1)
            act.activation(xp_sb[0:RX, :].rearrange("p (h t) -> p h t", t=HT), misc[0:RX, 0:2], ACT.Copy).then_inc(xp_evac, 1)
            act.wait_ge(xp_evac, 1)
            act.dma_start(xp_dram.rearrange("a n t -> (a n) t"), xp_sb[R:RX, :]).then_inc(xp_stored, 16)
            k_copy(0, 7, True)
            split_w(2, wk_hi)
            v_copy(0, 0, True)

            def softplus_exp(c):
                act.wait_ge(sp_max, c + 1)
                act.activation(w[:, c].rearrange("p (h t) -> p h t", t=HT), misc[:, 2 * (c % 2):2 * (c % 2) + 2], ACT.Abs,
                               bias=dtb[:, c:c + 1]).then_inc(sp_abs, 1)
                act.wait_ge(sp_abs, c + 1)
                act.activation(w[:, c], w[:, c], ACT.Exp, scale=-1.0).then_inc(sp_exp, 1)

            def softplus_log(c):
                act.wait_ge(sp_exp, c + 1)
                act.activation(u[:, c], w[:, c], ACT.Ln, bias=1.0).then_inc(sp_log, 1)

            softplus_exp(0)
            softplus_exp(1)
            v_copy(0, 1, True)
            softplus_exp(2)
            softplus_exp(3)
            softplus_log(0)
            v_copy(0, 2, True)
            softplus_log(1)
            softplus_log(2)
            act.wait_ge(xp_stored, 16)
            for n in range(2):
                load_bc(n, n)
            v_copy(0, 3, True)
            softplus_log(3)
            for b in range(4, B):
                v_copy(0, b, True)
            act.wait_ge(a_neg, 1)
            with act.Fori(1, SCANS) as g:
                group(g, TRI, TRI)
            group(SCANS, TRI, TRI - 1)
            group(SCANS + 1, REST, 0)
            g = NG - 1
            act.wait_ge(v_done, B * g)
            split_w(2 * g + 1, wv_hi)
            for j in range(K_LN2):
                k_copy(g, j)
            inverse_root(3, slice(0, B))
            for j in range(K_LN2, KZ):
                k_copy(g, j)

            def split_wq(g, p):
                act.wait_ge(wq_in[p], in_count(g, p, 16))
                if not known(g) or g > 1:
                    act.wait_ge(q_done, g - 1)
                act.activation(wq_hi[p][:], wq_raw[p][:], ACT.Copy).then_inc(wq_hi_done, 1)

            def split_wo(g, p):
                act.wait_ge(wo_in[p], in_count(g, p, 16))
                if not known(g) or g > 1:
                    act.wait_ge(o_done, g - 1)
                act.activation(wo_hi[p][:], wo_raw[p][:], ACT.Copy).then_inc(wo_hi_done, 1)

            def z_split(c):
                act.wait_ge(zt_ps, c + 1)
                act.activation(z_hi[:, c].rearrange("p (h t) -> p h t", t=HT), misc[:, 2 * (c % 2):2 * (c % 2) + 2], ACT.Copy,
                               scale=lnw[:, c:c + 1]).then_inc(z_hi_done, 1)

            copies = [(k_copy, j) for j in range(KZ, KP)] + [(v_copy, b) for b in range(2)]
            for c in range(C):
                z_split(c)
                copy, j = copies.pop(0)
                copy(g, j)
            split_wq(0, 0)
            for copy, j in copies:
                copy(g, j)

            def step(g, par, half):
                p = par % 2
                if runs(g):
                    act.wait_ge(q_done, g + 1)
                    if not known(g) or g > 1:
                        act.wait_ge(s_done, g - 1)
                    act.activation(q_sb[p][:], psQ, ACT.Copy).then_inc(q_evac, 1)
                if runs(g) and runs(g + 1):
                    split_wq(g + 1, 1 - p)
                if runs(g - 2):
                    split_wo(g - 2, p)
                if known(g) and g == STEPS + 1:
                    high_weff(range(2, 3))
                if runs(g - 1):
                    q = 1 - p
                    act.wait_ge(mx_done, g)
                    for b in range(HB):
                        last = act.activation(prob[q][:, b], prob[q][:, b], ACT.Exp, bias=negm[q][:, b:b + 1],
                                              accum_out=psum[q][:, b:b + 1])
                    last.then_inc(exp_done, 1)
                if runs(g - 2):
                    act.wait_ge(pv_done, g - 1)
                    if not known(g) or g > 3:
                        act.wait_ge(o_done, g - 3)
                    act.activation(ot_hi[p][:], psO, ACT.Copy).then_inc(ot_hi_done, 1)
                if known(g) and g == STEPS - 2:
                    inverse_root(4, slice(0, HB))
                if known(g) and g == STEPS:
                    high_weff(range(2))

            def high_weff(cs):
                for c in cs:
                    act.wait_ge(weff_sum, c + 1)
                    act.activation(weff_hi[:, c], ffn_w[:, c], ACT.Copy).then_inc(weff_hi_done, 1)

            def behind(g):
                if g <= 2:
                    for b in range(2 * g + 2, 2 * g + 4):
                        v_copy(NG - 1, b)

            pipeline(act, step, behind)

            high_weff(range(3, C))
            for half in range(2):
                bank = acc if half else misc
                for c in range(C):
                    act.wait_ge(zf_ps, C * half + c + 1)
                    act.activation(zf_hi[:, c, half * HT:(half + 1) * HT], bank[:, c], ACT.Copy).then_inc(zf_hi_done, 1)
                if half == 0:
                    inverse_root(5, slice(HB, B))

        @block.vector
        def _(dve):
            links = [0]

            def link(ins):
                links[0] += 1
                ins.then_inc(dve_chain, 1)
                dve.wait_ge(dve_chain, links[0])

            def moments(tile, bs):
                for b in bs:
                    last = dve.bn_stats(stats[:, b], tile[:, b])
                link(last)
                for b in bs:
                    last = dve.bn_aggr(mv[:, b], stats[:, b])
                link(last)

            def refine(n, part):
                dve.wait_ge(ln_exp, n)
                link(dve.tensor_tensor(tmp8[:, part], rstd[:, part], rstd[:, part], ALU.mult))
                link(dve.tensor_tensor(tmp8[:, part], tmp8[:, part], var[:, part], ALU.mult))
                link(dve.tensor_scalar(tmp8[:, part], tmp8[:, part], -0.5, 1.5, ALU.mult, ALU.add))
                link(dve.tensor_tensor(rstd[:, part], rstd[:, part], tmp8[:, part], ALU.mult))

            def norm(out, tile, b):
                return dve.tensor_scalar(out, tile, mv[:, b, 0:1], rstd[:, b:b + 1], ALU.subtract, ALU.mult)

            for c in range(C):
                dve.wait_ge(ctx_hi_done, c + 1)
                dve.tensor_tensor(ctx_lo[:, c], ctx_raw[:, c], ctx_hi[:, c].bitcast(F32), ALU.subtract).then_inc(ctx_lo_done, 1)
            everyone = slice(0, B)
            for i in range(2):
                dve.wait_ge(x_in[i], 16)
                moments(w_tok, range(HB * i, HB * (i + 1)))
            dve.tensor_scalar(var[:], mv[:, :, 1], EPS, None, ALU.add).then_inc(ln_var, 1)
            refine(1, everyone)
            for b in range(B):
                norm(w_tok[:, b], w_tok[:, b], b).then_inc(ln1_done, 1)
            dve.wait_ge(params_in, 16 * 7)
            dve.tensor_scalar(maskadd[:], maskraw[:], 1.0, -MASKED, ALU.subtract, ALU.mult).then_inc(mask_done, 1)
            dve.tensor_reduce(anykey[:], maskraw[:], AX_X, ALU.max).then_inc(mask_done, 1)
            def softplus_max(c):
                dve.wait_ge(dt_ps, c + 1)
                dve.tensor_scalar(dt_[:, c].rearrange("p (h t) -> p h t", t=HT), misc[:, 2 * (c % 2):2 * (c % 2) + 2],
                                  dtb[:, c:c + 1], 0.0, ALU.add, ALU.max).then_inc(sp_max, 1)

            def rest_of_one(c):
                e, v = w[:, c], v_tile[c]
                dve.wait_ge(sp_exp, c + 1)
                link(dve.tensor_scalar(v, e, 1.0, -1.0, ALU.add, ALU.add))
                dve.tensor_tensor(v, e, v, ALU.subtract).then_inc(sp_rest, 1)

            def softplus_sum(c):
                v = v_tile[c]
                dve.wait_ge(sp_rest, c + 1)
                dve.wait_ge(sp_log, c + 1)
                link(dve.tensor_tensor(v, v, u[:, c], ALU.add))
                dve.tensor_tensor(dt_[:, c], dt_[:, c], v, ALU.add).then_inc(sp_done, 1)

            v_tile = [dA[c][:, :, :].rearrange("p b s -> p (b s)") for c in range(2)] + [bc[2][:, c] for c in range(2)]
            softplus_max(0)
            softplus_max(1)
            rest_of_one(0)
            softplus_max(2)
            rest_of_one(1)
            softplus_max(3)
            rest_of_one(2)
            rest_of_one(3)
            for c in range(C):
                softplus_sum(c)
                if c < 2:
                    dve.wait_ge(sp_done, c + 1)
                    dve.memset(dA[c][:, :, 0:1], 0.0).then_inc(da_free, 1)

            def dbx(g, t, c):
                j = J * (g - 1) + C * t + c
                dve.wait_ge(y_ready, j + 1)
                if c == 0:
                    dve.wait_ge(bc_in[t], 16 * g)
                dve.tensor_tensor(w[:, c], u[:, c], bc[t][:, 0], ALU.mult).then_inc(dbx_done, 1)

            def scan_step(g, t, c):
                j = J * (g - 1) + C * t + c
                dve.wait_ge(dbx_done, j + 1)
                dve.wait_ge(da_ready, j + 1)
                dve.tensor_tensor_scan(w[:, c], dA[c % 2][:, :, :].rearrange("p b s -> p (b s)"), w[:, c], 0.0,
                                       ALU.mult, ALU.add).then_inc(da_free, 1)

            def times_c(g, t, c):
                j = J * (g - 1) + C * t + c
                dve.wait_ge(da_free, j + 3)
                dve.tensor_tensor(w[:, c], w[:, c], bc[t][:, 1], ALU.mult).then_inc(prod_done, 1)

            def states(g, count):
                steps = [(g, t, c) for t in range(count) for c in range(C)]
                dbx(*steps[0])
                for i, now in enumerate(steps):
                    if i + 1 < len(steps):
                        dbx(*steps[i + 1])
                    if i:
                        times_c(*steps[i - 1])
                    scan_step(*now)
                times_c(*steps[-1])

            with dve.Fori(1, SCANS + 1) as g:
                states(g, TRI)
            states(SCANS + 1, REST)

            dve.wait_ge(x_again, 16)
            for b in range(B):
                dve.wait_ge(yt_ps, b + 1)
                dve.tensor_tensor(base[:, b], base[:, b], misc[:, b % 4], ALU.add).then_inc(x1_done, 1)
            dve.wait_ge(x1_done, B)
            moments(base, range(B))
            dve.tensor_scalar(var[:], mv[:, :, 1], EPS, None, ALU.add).then_inc(ln_var, 1)
            refine(2, everyone)
            for b in range(B):
                last = norm(w_tok[:, b], base[:, b], b)
            link(last)
            moments(w_tok, range(B))
            link(dve.tensor_tensor(tmp8[:], mv[:, :, 0], mv[:, :, 0], ALU.mult))
            link(dve.tensor_tensor(tmp8[:], tmp8[:], mv[:, :, 1], ALU.add))
            dve.tensor_scalar(var[:], tmp8[:], EPS, None, ALU.add).then_inc(ln_var, 1)
            for b in range(B):
                last = dve.tensor_tensor(base[:, b], base[:, b], w_tok[:, b], ALU.add)
            link(last)
            refine(3, everyone)
            for b in range(B):
                dve.tensor_scalar(w_tok[:, b], w_tok[:, b], rstd[:, b:b + 1], None, ALU.mult).then_inc(zn_done, 1)
            for c in range(C):
                dve.wait_ge(z_hi_done, c + 1)
                dve.scalar_tensor_tensor(z_lo[:, c].rearrange("p (h t) -> p h t", t=HT), misc[:, 2 * (c % 2):2 * (c % 2) + 2],
                                         lnw[:, c:c + 1], z_hi[:, c].bitcast(F32).rearrange("p (h t) -> p h t", t=HT),
                                         ALU.mult, ALU.subtract).then_inc(z_lo_done, 1)

            def step(g, par, half):
                p = par % 2
                if runs(g - 2):
                    sh = (g - 2) // H if known(g) else half
                    dve.wait_ge(exp_done, g - 1)
                    dve.reciprocal(rec[p][:], psum[p][:]).then_inc(rec_done, 1)
                    dve.wait_ge(rec_done, g - 1)
                    dve.tensor_tensor(rec[p][:], rec[p][:], anykey[:, sh * HB:(sh + 1) * HB], ALU.mult).then_inc(recv_done, 1)
                    dve.wait_ge(recv_done, g - 1)
                    dve.tensor_tensor(prob[p][:], prob[p][:], rec[p][:, :].unsqueeze(2).to_broadcast([P, HB, S]),
                                      ALU.mult).then_inc(p_ready, 1)
                    if known(g) and g >= STEPS:
                        sum_weff(2 * (g - STEPS))
                    dve.wait_ge(t_done, g - 1)
                    if not known(g) or g > 3:
                        dve.wait_ge(pv_done, g - 3)
                    dve.tensor_copy(pt_sb[p][:, :, :].rearrange("p b q -> p (b q)"), psT).then_inc(pt_evac, 1)
                if runs(g - 1):
                    q = 1 - p
                    dve.wait_ge(s_done, g)
                    dve.wait_ge(bm_done, g)
                    if not known(g) or g > 2:
                        dve.wait_ge(t_done, g - 2)
                    dve.tensor_tensor(prob[q][:], psS.rearrange("p (b k) -> p b k", k=S), bm[q][:], ALU.add).then_inc(sb_done, 1)
                    dve.wait_ge(sb_done, g)
                    dve.tensor_reduce(negm[q][:], prob[q][:], AX_X, ALU.max, negate=True).then_inc(mx_done, 1)
                if known(g):
                    if g - 3 == H - 1:
                        add_sums(0)
                    if g == STEPS - 2:
                        moments_3(0)
                    if g == STEPS - 1:
                        norm_3(range(HB // 2))
                    if STEPS <= g <= STEPS + 1:
                        sum_weff(2 * (g - STEPS) + 1)
                    if g == STEPS:
                        norm_3(range(HB // 2, HB))
                    if g == STEPS + 1:
                        low_weff(range(2))
                if runs(g - 2):
                    dve.wait_ge(ot_hi_done, g - 1)
                    dve.tensor_tensor(ot_lo[p][:], psO, ot_hi[p][:].bitcast(F32), ALU.subtract).then_inc(ot_lo_done, 1)

            def add_sums(half):
                dve.wait_ge(o_done, (half + 1) * H)
                for b in range(HB):
                    dve.tensor_tensor(base[:, half * HB + b], base[:, half * HB + b], acc[:, b], ALU.add).then_inc(x2_done, 1)

            def sum_weff(c):
                dve.wait_ge(weff_ps, c + 1)
                dve.tensor_tensor(ffn_w[:, c], ffn_w[:, c], psQ, ALU.add).then_inc(weff_sum, 1)

            def low_weff(cs):
                for c in cs:
                    dve.wait_ge(weff_hi_done, c + 1)
                    dve.tensor_tensor(weff_lo[:, c], ffn_w[:, c], weff_hi[:, c].bitcast(F32), ALU.subtract).then_inc(weff_lo_done, 1)

            def moments_3(half):
                part = slice(half * HB, (half + 1) * HB)
                dve.wait_ge(x2_done, (half + 1) * HB)
                moments(base, range(half * HB, (half + 1) * HB))
                dve.tensor_scalar(var[:, part], mv[:, part, 1], EPS, None, ALU.add).then_inc(ln_var, 1)

            def norm_3(bs):
                if bs[0] % HB == 0:
                    refine(4 + bs[0] // HB, slice(bs[0], bs[0] + HB))
                for b in bs:
                    norm(xn[:, b], base[:, b], b).then_inc(ln3_done, 1)

            def f_split(half):
                bank = acc if half else misc
                for c in range(C):
                    dve.wait_ge(zf_hi_done, C * half + c + 1)
                    dve.tensor_tensor(zf_lo[:, c, half * HT:(half + 1) * HT], bank[:, c],
                                      zf_hi[:, c, half * HT:(half + 1) * HT].bitcast(F32), ALU.subtract).then_inc(zf_lo_done, 1)

            def finish(bs):
                for b in bs:
                    dve.wait_ge(bias_added, b + 1)
                    dve.wait_ge(f_done, b + 1)
                    dve.tensor_tensor(base[:, b], base[:, b], misc[:, b % HB], ALU.add).then_inc(out_ready, 1)

            pipeline(dve, step)
            low_weff(range(2, C))
            f_split(0)
            add_sums(1)
            moments_3(1)
            norm_3(range(HB, B))
            finish(range(2))
            f_split(1)
            finish(range(2, B))

        @block.gpsimd
        def _(pool):
            pool.memset(ident[:], 0.0).then_inc(ident_set, 1)
            pool.wait_ge(ident_set, 1)
            pool.affine_select(out=ident[:], in_=ident[:], compare_op=ALU.not_equal, fill=1.0, base=0,
                               pattern=[[-1, P]], channel_multiplier=1).then_inc(ident_done, 1)

            for c in range(C):
                pool.wait_ge(wk_hi_0, c + 1)
                pool.tensor_tensor(wk_lo[:, c], wraw[:, c], wk_hi[:, c].bitcast(F32), ALU.subtract).then_inc(wk_lo_0, 1)

            def low_w(m, hi, lo):
                pool.wait_ge(w_hi_done, m)
                pool.tensor_tensor(lo[:], wraw[:], hi[:].bitcast(F32), ALU.subtract).then_inc(w_lo_done, 1)

            def add_y(g, t, c):
                j = J * (g - 1) + C * t + c
                pool.wait_ge(prod_done, j + 1)
                pool.tensor_tensor(y[:, c], y[:, c], w[:, c], ALU.add).then_inc(y_ready, 1)

            def y_start(c):
                pool.wait_ge(sp_done, c + 1)
                pool.tensor_tensor(u[:, c], dt_[:, c], y[:, c], ALU.mult).then_inc(u_done, 1)
                pool.wait_ge(u_done, c + 1)
                pool.tensor_scalar(y[:, c], y[:, c], dskip[:, c:c + 1], 1.0, ALU.mult, ALU.mult).then_inc(y_ready, 1)

            low_w(1, wv_hi, wv_lo)
            low_w(2, wk_hi, wk_lo)
            pool.wait_ge(params_in, 16 * 7)
            for c in range(C):
                y_start(c)
            with pool.Fori(1, SCANS + 1) as g:
                low_w(2 * g + 1, wv_hi, wv_lo)
                for i in range(J):
                    if i == J // 2:
                        low_w(2 * g + 2, wk_hi, wk_lo)
                    add_y(g, i // C, i % C)
            low_w(2 * NG - 3, wv_hi, wv_lo)
            for c in range(C * REST):
                add_y(NG - 2, c // C, c % C)
            low_w(2 * NG - 2, wk_hi, wk_lo)
            low_w(2 * NG - 1, wv_hi, wv_lo)

            def low_wq(g, p):
                pool.wait_ge(wq_hi_done, g + 1)
                pool.tensor_tensor(wq_lo[p][:], wq_raw[p][:], wq_hi[p][:].bitcast(F32), ALU.subtract).then_inc(wq_lo_done, 1)

            low_wq(0, 0)

            def step(g, par, half):
                p = par % 2
                if runs(g) and runs(g + 1):
                    low_wq(g + 1, 1 - p)
                if runs(g):
                    sh = g // H if known(g) else half
                    if known(g) and g == 0:
                        pool.wait_ge(mask_done, 1)
                    pool.wait_ge(kb_in[p], in_count(g, p, 32))
                    if not known(g) or g >= 2:
                        pool.wait_ge(sb_done, g - 1)
                    pool.tensor_tensor(bm[p][:], bias[p][:, :].unsqueeze(1).to_broadcast([P, HB, S]),
                                       maskadd[:, sh * HB:(sh + 1) * HB], ALU.add).then_inc(bm_done, 1)
                if runs(g - 2):
                    pool.wait_ge(wo_hi_done, g - 1)
                    pool.tensor_tensor(wo_lo[p][:], wo_raw[p][:], wo_hi[p][:].bitcast(F32), ALU.subtract).then_inc(wo_lo_done, 1)

            def step_and_tail(g, par, half):
                step(g, par, half)
                if known(g) and g == H:
                    pool.wait_ge(ffn_in, 16 * 6)
                    for e in range(ER):
                        pool.tensor_scalar(eb_sb[:, e], eb_sb[:, e], eprob[:, e:e + 1], 1.0, ALU.mult, ALU.mult).then_inc(eb_done, 1)

                if known(g) and STEPS <= g <= STEPS + 1:
                    add_bias(0, range(2 * (g - STEPS), 2 * (g - STEPS) + 2))

            def add_bias(half, bs):
                pool.wait_ge(ln3_done, (half + 1) * HB)
                for b in bs:
                    b += half * HB
                    pool.tensor_tensor(base[:, b], base[:, b], ffn_b[:], ALU.add).then_inc(bias_added, 1)

            pipeline(pool, step_and_tail)
            add_bias(1, range(HB))


def kernel(**inputs):
    import numpy as np
    import concourse.bacc as bacc
    from concourse.bass_utils import run_bass_kernel_spmd as run

    x = np.asarray(inputs["x"])

    def chunks(m):
        m = np.asarray(m)
        return m.reshape(m.shape[0] // P, P, -1).transpose(1, 0, 2)

    def groups(m, heads):
        m = np.asarray(m)
        return m.reshape(H // heads, heads * P, C, P).transpose(0, 3, 2, 1)

    arrays = {
        "x": x,
        "ctxT": chunks(np.asarray(inputs["ctx_4096"]).reshape(T, D).T),
        "mask": inputs["mask_BxSxS2_bk0"],
        "A_log": chunks(inputs["L0_attn_A_log"]),
        "D": np.asarray(inputs["L0_attn_D"]).reshape(C, P).T,
        "dt_b": np.asarray(inputs["L0_attn_dt_proj_b"]).reshape(C, P).T,
        "xp_w": chunks(np.asarray(inputs["L0_attn_x_proj_w"]).T),
        "dt_w": np.asarray(inputs["L0_attn_dt_proj_w"]).T,
        "ln_w": np.asarray(inputs["L0_xattn_ln_weight"]).reshape(C, P).T,
        "pbias": inputs["L0_xattn_position_bias"],
        "wq": groups(inputs["L0_xattn_w_q"], 1),
        "wk": groups(inputs["L0_xattn_w_k"], G),
        "wv": groups(inputs["L0_xattn_w_v"], G),
        "wo": np.asarray(inputs["L0_xattn_w_out"]).T.reshape(H, P, D),
        "ffn_w": chunks(np.asarray(inputs["L0_ffn_W"]).T),
        "ffn_a": chunks(np.asarray(inputs["L0_ffn_A"]).reshape(-1, D)),
        "ffn_bw": chunks(np.asarray(inputs["L0_ffn_B"]).transpose(0, 2, 1).reshape(-1, D)),
        "ffn_b": inputs["L0_ffn_b"],
        "probs": np.repeat(np.asarray(inputs["L0_ffn_probs"]), P * ER // E).reshape(-1, 1),
    }
    nc = bacc.Bacc("TRN2", target_bir_lowering=False, num_devices=1)
    a, given = {}, {}
    for name, v in arrays.items():
        v = np.ascontiguousarray(v)
        given[f"in_{name}"] = v
        a[name] = nc.dram_tensor(f"in_{name}", v.shape, mybir.dt.from_np(v.dtype), kind="ExternalInput").ap()
    a["out"] = nc.dram_tensor("out_x", x.shape, F32, kind="ExternalOutput").ap()
    decoder_layer(nc, a)
    r = run(nc, [given], core_ids=[0])
    return r.results[0]["out_x"]
```
